# Optimizing a Trainium2 kernel written in Bass

```python
import numpy as np
import jax
import jax.numpy as jnp

def _softmax(x, axis=-1):
    return jax.nn.softmax(x, axis=axis)

def _gelu(x):
    return jax.nn.gelu(x, approximate=True)

def _silu(x):
    return jax.nn.silu(x)

def _sigmoid(x):
    return jax.nn.sigmoid(x)

def _layernorm(x, axis=-1, eps=1e-05):
    m = jnp.mean(x, axis=axis, keepdims=True)
    v = jnp.var(x, axis=axis, keepdims=True)
    return (x - m) / jnp.sqrt(v + eps)

def _scatter_add(tgt, idx, src, axis=0):
    return tgt.at[idx].add(src)

def _segment_sum(src, seg, n):
    return jax.ops.segment_sum(src, seg, n)
kernel_name = 'mk_gnn_preln_d2_gnn_r32_fd4704'

def setup_inputs(seed: int=0):
    np.random.seed(seed)
    _w = jnp.asarray

    def _rec_inputs():
        import jax
        import jax.numpy as jnp
        _gk = jax.random.key(seed)
        x = -8.776e-05 + 1 * jax.random.normal(jax.random.fold_in(_gk, 1), (3125, 128), jnp.float32)
        _s = jax.random.randint(jax.random.fold_in(_gk, 2), (50000,), 0, 3125, jnp.int32)
        _d = jax.random.randint(jax.random.fold_in(_gk, 3), (50000,), 0, 3125, jnp.int32)
        _loop = jnp.arange(3125, dtype=jnp.int32)
        src = jnp.concatenate([_s, _d, _loop])
        dst = jnp.concatenate([_d, _s, _loop])
        _o = jnp.argsort(dst, stable=True)
        src = src[_o]
        dst = dst[_o]
        edge_attr_4 = 0.0012443 + 1.0001 * jax.random.normal(jax.random.fold_in(_gk, 12), (103125, 4), jnp.float32)
        edge_attr_8 = -0.000521468 + 0.999954 * jax.random.normal(jax.random.fold_in(_gk, 13), (103125, 8), jnp.float32)
        edge_type_32 = jax.random.randint(jax.random.fold_in(_gk, 14), (103125,), 0, 32, jnp.int32)
        edge_weight1 = jax.random.uniform(jax.random.fold_in(_gk, 15), (103125, 1), jnp.float32, 0.0, 0.999998)
        node_vec1 = jax.random.uniform(jax.random.fold_in(_gk, 16), (3125, 1), jnp.float32, 0.0, 1)
        return (x, src, dst, edge_attr_4, edge_attr_8, edge_type_32, edge_weight1, node_vec1)
    x, src, dst, edge_attr_4, edge_attr_8, edge_type_32, edge_weight1, node_vec1 = _rec_inputs()

    def _L0_gnn_setup():
        import jax, jax.numpy as jnp
        import numpy as np
        N_NODES = 1250
        N_EDGES = 20000
        MUL = 32
        NUM_NEIGHBORS = 16.0
        SILU_NORM = 1.6791767923989418
        SQRT3 = 3.0 ** 0.5
        key = jax.random.key(seed)
        ks = jax.random.split(key, 12)
        return {'node_input': jax.random.normal(ks[0], (N_NODES, 4 * MUL), dtype=jnp.float32), 'node_attr': jnp.ones((N_NODES, 1), dtype=jnp.float32), 'edge_src': jax.random.randint(ks[1], (N_EDGES,), 0, N_NODES, dtype=jnp.int32), 'edge_dst': jax.random.randint(ks[2], (N_EDGES,), 0, N_NODES, dtype=jnp.int32), 'edge_attr': jax.random.normal(ks[3], (N_EDGES, 4), dtype=jnp.float32), 'edge_scalars': jax.random.normal(ks[4], (N_EDGES, 8), dtype=jnp.float32), 'w_lin1_s': jax.random.normal(ks[5], (MUL, MUL), dtype=jnp.float32), 'w_lin1_v': jax.random.normal(ks[6], (MUL, MUL), dtype=jnp.float32), 'fc_w1': jax.random.normal(ks[7], (8, 64), dtype=jnp.float32), 'fc_w2': jax.random.normal(ks[8], (64, 4 * MUL), dtype=jnp.float32), 'w_lin2_s': jax.random.normal(ks[9], (2 * MUL, MUL), dtype=jnp.float32), 'w_lin2_v': jax.random.normal(ks[10], (2 * MUL, MUL), dtype=jnp.float32)}
    _L0_gnn_all = _L0_gnn_setup()
    _L0_gnn_in = {k: v for k, v in _L0_gnn_all.items() if k in ('w_lin1_s', 'w_lin1_v', 'fc_w1', 'fc_w2', 'w_lin2_s', 'w_lin2_v')}
    del _L0_gnn_all

    def _L1_gnn_setup():
        import jax, jax.numpy as jnp
        import numpy as np
        N_NODES = 50000
        N_EDGES = 15625
        IN_FEAT = 128
        OUT_FEAT = 128
        NUM_RELS = 32
        NUM_BASES = 8
        key = jax.random.key(seed)
        ks = jax.random.split(key, 8)
        h = jax.random.normal(ks[0], (N_NODES, IN_FEAT), dtype=jnp.float32)
        src = jax.random.randint(ks[1], (N_EDGES,), 0, N_NODES, dtype=jnp.int32)
        dst = jax.random.randint(ks[2], (N_EDGES,), 0, N_NODES, dtype=jnp.int32)
        etype = jax.random.randint(ks[3], (N_EDGES,), 0, NUM_RELS, dtype=jnp.int32)
        norm = jax.random.uniform(ks[4], (N_EDGES, 1), dtype=jnp.float32)
        weight = jax.random.normal(ks[5], (NUM_BASES, IN_FEAT, OUT_FEAT), dtype=jnp.float32) * 0.05
        w_comp = jax.random.normal(ks[6], (NUM_RELS, NUM_BASES), dtype=jnp.float32) * 0.3
        bias_param = jax.random.normal(ks[7], (OUT_FEAT,), dtype=jnp.float32) * 0.05
        return {'h': h, 'src': src, 'dst': dst, 'etype': etype, 'norm': norm, 'weight': weight, 'w_comp': w_comp, 'bias_param': bias_param}
    _L1_gnn_all = _L1_gnn_setup()
    _L1_gnn_in = {k: v for k, v in _L1_gnn_all.items() if k in ('weight', 'w_comp', 'bias_param')}
    del _L1_gnn_all
    return {'x': x, 'src': src, 'dst': dst, 'edge_attr_4': edge_attr_4, 'edge_attr_8': edge_attr_8, 'edge_type_32': edge_type_32, 'edge_weight1': edge_weight1, 'node_vec1': node_vec1, 'L0_gnn_w_lin1_s': _L0_gnn_in['w_lin1_s'], 'L0_gnn_w_lin1_v': _L0_gnn_in['w_lin1_v'], 'L0_gnn_fc_w1': _L0_gnn_in['fc_w1'], 'L0_gnn_fc_w2': _L0_gnn_in['fc_w2'], 'L0_gnn_w_lin2_s': _L0_gnn_in['w_lin2_s'], 'L0_gnn_w_lin2_v': _L0_gnn_in['w_lin2_v'], 'L1_gnn_weight': _L1_gnn_in['weight'], 'L1_gnn_w_comp': _L1_gnn_in['w_comp'], 'L1_gnn_bias_param': _L1_gnn_in['bias_param']}

def reference(x, src, dst, edge_attr_4, edge_attr_8, edge_type_32, edge_weight1, node_vec1, L0_gnn_w_lin1_s, L0_gnn_w_lin1_v, L0_gnn_fc_w1, L0_gnn_fc_w2, L0_gnn_w_lin2_s, L0_gnn_w_lin2_v, L1_gnn_weight, L1_gnn_w_comp, L1_gnn_bias_param):
    import jax
    import jax.numpy as jnp

    def _L0_gnn_ref(node_input, node_attr, edge_src, edge_dst, edge_attr, edge_scalars, w_lin1_s, w_lin1_v, fc_w1, fc_w2, w_lin2_s, w_lin2_v):
        import jax, jax.numpy as jnp
        import numpy as np
        N_NODES = 1250
        N_EDGES = 20000
        MUL = 32
        NUM_NEIGHBORS = 16.0
        SILU_NORM = 1.6791767923989418
        SQRT3 = 3.0 ** 0.5
        N = node_input.shape[0]
        s = node_input[:, :MUL]
        v = node_input[:, MUL:].reshape(N, MUL, 3)
        s = s @ (w_lin1_s / jnp.sqrt(jnp.float32(MUL)))
        v = jnp.einsum('nui,uw->nwi', v, w_lin1_v / jnp.sqrt(jnp.float32(MUL)))
        h = jax.nn.silu(edge_scalars @ (fc_w1 / jnp.sqrt(jnp.float32(fc_w1.shape[0])))) * SILU_NORM
        w = h @ (fc_w2 / jnp.sqrt(jnp.float32(fc_w2.shape[0])))
        w0 = w[:, 0 * MUL:1 * MUL]
        w1 = w[:, 1 * MUL:2 * MUL]
        w2 = w[:, 2 * MUL:3 * MUL]
        w3 = w[:, 3 * MUL:4 * MUL]
        se = s[edge_src]
        ve = v[edge_src]
        es = edge_attr[:, :1]
        ev = edge_attr[:, 1:4]
        mid_s0 = w0 * se * es
        mid_s1 = w3 * jnp.einsum('eui,ei->eu', ve, ev) / SQRT3
        mid_v0 = (w1 * se)[:, :, None] * ev[:, None, :]
        mid_v1 = (w2 * es)[:, :, None] * ve
        mid_scal = jnp.concatenate([mid_s0, mid_s1], axis=1)
        mid_vec = jnp.concatenate([mid_v0, mid_v1], axis=1)
        inv = 1.0 / jnp.sqrt(jnp.float32(NUM_NEIGHBORS))
        ns = jax.ops.segment_sum(mid_scal, edge_dst, num_segments=N) * inv
        nv = jax.ops.segment_sum(mid_vec, edge_dst, num_segments=N) * inv
        fan = jnp.sqrt(jnp.float32(2 * MUL))
        out_s = ns @ (w_lin2_s / fan)
        out_v = jnp.einsum('nui,uw->nwi', nv, w_lin2_v / fan)
        return jnp.concatenate([out_s, out_v.reshape(N, -1)], axis=1)

    def _L1_gnn_ref(h, src, dst, etype, norm, weight, w_comp, bias_param):
        import jax, jax.numpy as jnp
        import numpy as np
        N_NODES = 50000
        N_EDGES = 15625
        IN_FEAT = 128
        OUT_FEAT = 128
        NUM_RELS = 32
        NUM_BASES = 8
        hsrc = h[src]
        coef = w_comp[etype]
        msg = jnp.zeros((hsrc.shape[0], weight.shape[2]), dtype=h.dtype)
        for b in range(weight.shape[0]):
            msg = msg + hsrc @ weight[b] * coef[:, b][:, None]
        msg = msg * norm
        node_repr = jax.ops.segment_sum(msg, dst, num_segments=h.shape[0])
        node_repr = node_repr + bias_param
        return jax.nn.relu(node_repr)
    h = jnp.maximum(_layernorm(x, axis=-1), 0.0)
    x = x + _L0_gnn_ref(h, node_vec1, src, dst, edge_attr_4, edge_attr_8, L0_gnn_w_lin1_s, L0_gnn_w_lin1_v, L0_gnn_fc_w1, L0_gnn_fc_w2, L0_gnn_w_lin2_s, L0_gnn_w_lin2_v)
    h = jnp.maximum(_layernorm(x, axis=-1), 0.0)
    x = x + _L1_gnn_ref(h, src, dst, edge_type_32, edge_weight1, L1_gnn_weight, L1_gnn_w_comp, L1_gnn_bias_param)
    return x

_drawn_inputs = setup_inputs


def setup_inputs(seed=0):
    import zlib

    import numpy as np

    out = dict(_drawn_inputs(seed))
    spreads = {}
    factors = {}
    for name, (base, spread) in spreads.items():
        noise = np.random.default_rng([zlib.crc32(name.encode()), seed]).standard_normal(out[name].shape)
        drawn = base * np.exp(spread * noise) if base else spread * noise
        out[name] = jnp.asarray(drawn.astype(out[name].dtype))
    for name, factor in factors.items():
        out[name] = (out[name] * factor).astype(out[name].dtype)
    return out
```

```python
import concourse.bass as bass
from concourse import mybir
from contextlib import ExitStack

FP32 = mybir.dt.float32
BF16 = mybir.dt.bfloat16
I32 = mybir.dt.int32
ALU = mybir.AluOpType
ACT = mybir.ActivationFunctionType
AX = mybir.AxisListType

NODES = 3125
FEAT = 128
EDGES = 103125
MUL = 32
HID = 64
BASES = 8
RELS = 32

NB = 125
BLOCKS = NODES // NB
GB = 5
GROUPS = BLOCKS // GB

WIN = 32
HALF = 512
K = HALF // 128
H = 2
TILES = H * K
CHUNK = H * HALF
CHUNKS = -(-EDGES // CHUNK)
TAIL = EDGES - (CHUNKS - 1) * CHUNK
TAIL1 = TAIL - HALF
LAST = CHUNKS - 1
PAIRS = CHUNKS // 2
assert HALF < TAIL < CHUNK and CHUNKS % 2 == 1 and CHUNKS <= 128
WINDOWS = -(-NODES // WIN)
ACC_N = NODES + WIN - 1

COEF = 4
QA = 4
QB = 3
Q = QA + QB

EPS = 1e-5
SILU_NORM = 1.6791767923989418
NUM_NEIGHBORS = 16.0
FC1_SCALE = 8 ** -0.5
LIN2_SCALE = MUL ** -0.5 * SILU_NORM * HID ** -0.5 * NUM_NEIGHBORS ** -0.5 * (2 * MUL) ** -0.5
INV_SQRT3 = 3.0 ** -0.5
PAD_LOW = -1.0
PAD_HIGH = 8192.0


def gnn_two_layers(nc, x, src, dst, ea4, ea8, etype, eweight, lin1_s, lin1_v, fc1, fc2, lin2_s, lin2_v,
                   weight, w_comp, bias, table0, table1, out):
    ctx = ExitStack()
    with ctx:
        def sb(name, shape, dt):
            return ctx.enter_context(nc.sbuf_tensor(name, shape, dt))

        def sem(name):
            return ctx.enter_context(nc.semaphore(name))

        ident = sb("ident", [128, 128], FP32)
        ident_bf = sb("ident_bf", [128, 128], BF16)
        iota_i = sb("iota_i", [128, WIN], I32)
        iota_w = sb("iota_w", [128, WIN], FP32)
        rel_i = sb("rel_i", [128, 1], I32)
        rel_id = sb("rel_id", [128, 1], FP32)
        ones = sb("ones", [128, 128], FP32)

        lin1 = sb("lin1", [FEAT, FEAT], FP32)
        fc1_bd = sb("fc1_bd", [TILES * 8, TILES // 2, 128], FP32)
        fc2_bd = sb("fc2_bd", [128, 256], FP32)
        lin2_a = sb("lin2_a", [128, MUL], FP32)
        lin2_b = sb("lin2_b", [128, MUL], FP32)
        lin2 = sb("lin2", [128, Q, FEAT], FP32)
        wc_bd = sb("wc_bd", [128, K * BASES], FP32)
        w_base = sb("w_base", [FEAT, BASES, FEAT], FP32)
        bias_b = sb("bias_b", [NB, FEAT], FP32)

        xs = sb("xs", [NB, BLOCKS, FEAT], FP32)
        stats = sb("stats", [NB, GB, 6], FP32)
        mv = sb("mv", [NB, BLOCKS, 2], FP32)
        var_eps = sb("var_eps", [NB, BLOCKS], FP32)
        std = sb("std", [NB, BLOCKS], FP32)
        rstd = sb("rstd", [NB, BLOCKS], FP32)
        nmr = sb("nmr", [NB, BLOCKS], FP32)
        hn = sb("hn", [NB, 2, GB, FEAT], FP32)
        hT = sb("hT", [FEAT, 2, GB, NB], FP32)
        rows_out = sb("rows_out", [NB, 2, GB, FEAT], FP32)
        ybias = sb("ybias", [NB, GB, FEAT], FP32)
        acc = sb("acc", [128, BASES, ACC_N], FP32)

        src_t = sb("src_t", [128, CHUNKS, TILES], I32)
        rel_t = sb("rel_t", [128, CHUNKS, TILES], FP32)
        ew_t = sb("ew_t", [128, CHUNKS, TILES], FP32)
        et_rows = sb("et_rows", [CHUNKS, CHUNK], BF16)
        wmin_f = sb("wmin_f", [1, CHUNKS, H], FP32)
        wmin = sb("wmin", [1, CHUNKS, H], I32)
        dmax = sb("dmax", [CHUNKS, H], FP32)
        dmin = sb("dmin", [CHUNKS, H], FP32)
        span = sb("span", [CHUNKS, H], FP32)
        wide = sb("wide", [CHUNKS, H], FP32)
        nwide = sb("nwide", [CHUNKS, 1], FP32)
        narrow = sb("narrow", [128, 1], FP32)
        general_f = sb("general_f", [1, 1], FP32)
        general = sb("general", [1, 1], I32)

        ea8_c = sb("ea8_c", [128, 2, H, K * 8], FP32)
        ea4_c = sb("ea4_c", [128, 2, H, K * COEF], FP32)
        idx_c = sb("idx_c", [128, 2, TILES], I32)
        got = sb("got", [128, 2, TILES, FEAT], FP32)
        xT = sb("xT", [TILES * 8, 2, 128], FP32)
        hid = sb("hid", [128, 2, TILES // 2, 128], FP32)
        onehot = sb("onehot", [128, 2, TILES, WIN], FP32)
        prod = sb("prod", [128, 2, TILES, 256], FP32)
        oc = sb("oc", [128, 2, TILES * BASES * WIN], FP32)
        sel_c = sb("sel_c", [CHUNKS, 2, 32], BF16)
        typ1 = sb("typ1", [128, 2, H * 128], FP32)
        coef = sb("coef", [128, 2, TILES, BASES], FP32)

        rows = prod[0:CHUNKS, :, :, :].rearrange("c a t f -> c (a t f)")
        src_f = rows[:, 0:1024]
        src_i = rows[:, 1024:2048].bitcast(I32)
        dst_i = rows[:, 2048:3072].bitcast(I32)
        ew_f = rows[:, 3072:4096]
        rows2 = oc[0:CHUNKS, :, :].rearrange("c a t -> c (a t)")
        dst_f = rows2[:, 0:1024]
        dst_hi = rows2[:, 1024:2048]
        et_i = rows2[:, 2048:3072].bitcast(I32)

        psum = ctx.enter_context(nc.psum_tensor("psum", [128, 8, 512], FP32))

        w_in = sem("w_in")
        lin1_in = sem("lin1_in")
        x_in = [sem(f"x_in{g}") for g in range(GROUPS)]
        e_in = sem("e_in")
        zeroed = sem("zeroed")
        id0 = sem("id0")
        const = sem("const")
        acc0_zero = sem("acc0_zero")
        consts_f = sem("consts_f")
        stat = sem("stat")
        aggr = sem("aggr")
        vared = sem("vared")
        rooted = sem("rooted")
        inv = sem("inv")
        nmred = sem("nmred")
        normed = sem("normed")
        tp_done = sem("tp_done")
        hT_copied = sem("hT_copied")
        t0_mm = sem("t0_mm")
        t0_rows = sem("t0_rows")
        t0_out = [sem("t0_out0"), sem("t0_out1")]
        lin2_ready = sem("lin2_ready")
        d_step = sem("d_step")
        d_rows = sem("d_rows")
        tr_done = sem("tr_done")
        tr_copied = sem("tr_copied")
        cnt_done = sem("cnt_done")
        min_done = sem("min_done")
        shifted = sem("shifted")
        tables = sem("tables")
        tables1 = sem("tables1")
        ea8_in = [sem("ea8_in0"), sem("ea8_in1")]
        ea4_in = [sem("ea4_in0"), sem("ea4_in1")]

        class Pass:
            def __init__(self, n):
                self.idx_ready = sem(f"idx_ready{n}")
                self.gathered = [sem(f"gathered{n}_0"), sem(f"gathered{n}_1")]
                self.onehot = sem(f"onehot{n}")
                self.oc_done = sem(f"oc_done{n}")
                self.agg_done = sem(f"agg_done{n}")
                self.acc_done = sem(f"acc_done{n}")
                self.round_done = sem(f"round_done{n}")

        p0, p1 = Pass(0), Pass(1)
        gather_turn = sem("gather_turn")
        turn_turn = sem("turn_turn")
        xT_done = sem("xT_done")
        xT_copied = sem("xT_copied")
        hid_done = sem("hid_done")
        silu_done = sem("silu_done")
        w_done = sem("w_done")
        prod_done = sem("prod_done")
        sel_ready = sem("sel_ready")
        typ_done = sem("typ_done")
        typ1_done = sem("typ1_done")
        cf_done = sem("cf_done")
        coef_done = sem("coef_done")
        l0_mm = sem("l0_mm")
        l0_add = sem("l0_add")
        n1_stat = sem("n1_stat")
        n1_aggr = sem("n1_aggr")
        n1_var = sem("n1_var")
        n1_root = sem("n1_root")
        n1_inv = sem("n1_inv")
        n1_nmr = sem("n1_nmr")
        n1_normed = sem("n1_normed")
        t1_out = [sem("t1_out0"), sem("t1_out1")]
        acc1_zero = sem("acc1_zero")
        l1_mm = sem("l1_mm")
        l1_bias = sem("l1_bias")
        l1_rows = sem("l1_rows")
        y_out = [sem("y_out0"), sem("y_out1")]

        N_WEIGHTS = TILES + 2 + 8 + K + 2 + 1
        EARLY_POOL = 5

        IN_BANKS = ((0, 3), (3, 2))

        def in_bank(bank, n):
            return psum[:, bank, 0:n * 128].rearrange("p (b f) -> p b f", b=n)

        def blocks_of(t, g, n=GB):
            return t.rearrange("(b p) f -> p b f", p=NB)[:, bass.ds(g * GB, n), :]

        def chunks_done(i, r):
            return r * CHUNKS + i + 1

        def slot_uses(slot, m, r):
            return r * (PAIRS + 1 - slot) + m + 1

        def ea_loads(slot, m, r, loads):
            return 16 * (r * (PAIRS + 3 if slot == 0 else PAIRS) + m + loads)

        def pairs(eng, first, body, last):
            first(0, 0, 0)
            first(1, 1, 0)
            with eng.Fori(1, PAIRS) as m:
                for s in range(2):
                    body(m * 2 + s, s, m)
            last(LAST, 0, PAIRS)

        block = ctx.enter_context(nc.Block())

        @block.sync
        def _(sp):
            for g in range(GROUPS):
                sp.dma_start(xs[:, g * GB:(g + 1) * GB, :], blocks_of(x, g)).then_inc(x_in[g], 16)
            sp.wait_ge(zeroed, EARLY_POOL)
            sp.wait_ge(id0, 3)
            sp.dma_start(lin1[0:MUL, 0:MUL], lin1_s).then_inc(lin1_in, 16)
            for i in range(3):
                sp.dma_start(lin1[MUL + i:FEAT:3, MUL * (i + 1):MUL * (i + 2)], lin1_v).then_inc(lin1_in, 16)
            full = LAST * CHUNK
            for row, t in ((src_i, src), (dst_i, dst), (ew_f, eweight), (et_i, etype)):
                sp.dma_start(row[0:LAST, :], t[0:full].rearrange("(c e) -> c e", e=CHUNK)).then_inc(e_in, 16)
                sp.dma_start(row[LAST:CHUNKS, 0:TAIL], t[full:EDGES].rearrange("(c e) -> c e", c=1)).then_inc(e_in, 16)
            for t in range(TILES):
                sp.dma_start(fc1_bd[8 * t:8 * t + 8, t // 2, HID * (t % 2):HID * (t % 2 + 1)], fc1).then_inc(w_in, 16)
            for n in range(2):
                sp.dma_start(fc2_bd[HID * n:HID * (n + 1), 128 * n:128 * (n + 1)], fc2).then_inc(w_in, 16)
            s0, s1 = lin2_s[0:MUL, :], lin2_s[MUL:2 * MUL, :]
            v0, v1 = lin2_v[0:MUL, :], lin2_v[MUL:2 * MUL, :]
            for n, (a, b) in enumerate(((s0, v1), (v0, s1), (v1, v1), (s1, s1))):
                sp.dma_start(lin2_a[MUL * n:MUL * (n + 1), :], a).then_inc(w_in, 16)
                sp.dma_start(lin2_b[MUL * n:MUL * (n + 1), :], b).then_inc(w_in, 16)
            for g in range(K):
                sp.dma_start(wc_bd[RELS * g:RELS * (g + 1), BASES * g:BASES * (g + 1)], w_comp).then_inc(w_in, 16)
            sp.dma_start(w_base[:, 0:4, :], weight[0:4].rearrange("b i o -> i b o")).then_inc(w_in, 16)
            sp.dma_start(w_base[:, 4:8, :], weight[4:8].rearrange("b i o -> i b o")).then_inc(w_in, 16)
            sp.dma_start(bias_b[:, :], bias.rearrange("(a f) -> a f", a=1).to_broadcast([NB, FEAT])).then_inc(w_in, 16)

            for g in range(GROUPS):
                sp.wait_ge(t0_rows, 2 * (g + 1))
                sp.dma_start(blocks_of(table0, g), rows_out[:, g % 2, :, :]).then_inc(t0_out[g % 2], 16)

            def load(i, s, m, r):
                a8 = ea8[bass.ds(i * CHUNK, CHUNK), :].rearrange("(h p k) c -> p h (k c)", h=H, k=K)
                a4 = ea4[bass.ds(i * CHUNK, CHUNK), :].rearrange("(h p k) c -> p h (k c)", h=H, k=K)
                sp.dma_start(ea8_c[:, s, :, :], a8).then_inc(ea8_in[s], 16)
                sp.dma_start(ea4_c[:, s, :, :], a4).then_inc(ea4_in[s], 16)

            def load_after(i, s, m, r):
                sp.wait_ge(xT_done, chunks_done(i - 2, r))
                sp.wait_ge(p0.oc_done, chunks_done(i - 2, r))
                load(i, s, m, r)

            def load_last(r):
                sp.wait_ge(xT_done, chunks_done(LAST - 2, r))
                sp.wait_ge(p0.oc_done, chunks_done(LAST - 2, r))
                a, b, e = LAST * CHUNK, LAST * CHUNK + HALF, EDGES - EDGES % K
                for t, c, buf, s_in in ((ea8, 8, ea8_c, ea8_in[0]), (ea4, COEF, ea4_c, ea4_in[0])):
                    sp.dma_start(buf[:, 0, 0, :], t[a:b, :].rearrange("(p k) c -> p (k c)", k=K)).then_inc(s_in, 16)
                    sp.dma_start(buf[0:TAIL1 // K, 0, 1, :], t[b:e, :].rearrange("(p k) c -> p (k c)", k=K)).then_inc(s_in, 16)
                    sp.dma_start(buf[TAIL1 // K:TAIL1 // K + 1, 0, 1, 0:(TAIL1 % K) * c],
                                 t[e:EDGES, :].rearrange("(p k) c -> p (k c)", p=1)).then_inc(s_in, 16)

            def load_pass(r):
                load(0, 0, 0, r)
                load(1, 1, 0, r)
                with sp.Fori(1, PAIRS) as m:
                    for s in range(2):
                        load_after(m * 2 + s, s, m, r)
                load_last(r)

            load_pass(0)
            sp.wait_ge(tables, 1)
            many = sp.value_load(general[0:1, 0:1], min_val=0, max_val=1)
            with sp.If(many > 0):
                with sp.Fori(1, WINDOWS) as r:
                    sp.wait_ge(tables, r + 1)
                    load_pass(r)

            for g in range(GROUPS):
                sp.wait_ge(n1_normed, (g + 1) * GB)
                sp.dma_start(blocks_of(table1, g), hn[:, g % 2, :, :]).then_inc(t1_out[g % 2], 16)
            for g in range(GROUPS):
                sp.wait_ge(l1_rows, (g + 1) * GB)
                sp.dma_start(blocks_of(out, g), rows_out[:, g % 2, :, :]).then_inc(y_out[g % 2], 16)
            sp.wait_ge(y_out[0], 16 * 3)
            sp.wait_ge(y_out[1], 16 * 2)

        @block.gpsimd
        def _(pool):
            nc.gpsimd.memset(lin1[:, :], 0.0).then_inc(zeroed, 1)
            nc.gpsimd.memset(fc1_bd[:, :, :], 0.0).then_inc(zeroed, 1)
            nc.gpsimd.memset(fc2_bd[:, :], 0.0).then_inc(zeroed, 1)
            nc.gpsimd.memset(wc_bd[:, :], 0.0).then_inc(zeroed, 1)
            pool.wait_ge(zeroed, 4)
            nc.gpsimd.memset(prod[96:CHUNKS, :, :, :], 0.0).then_inc(id0, 1)
            pool.wait_ge(id0, 1)
            nc.gpsimd.memset(dst_i[96:CHUNKS, :], int(PAD_LOW)).then_inc(id0, 1)
            pool.wait_ge(id0, 2)
            nc.gpsimd.memset(et_i[96:CHUNKS, :], 0).then_inc(id0, 1)
            pool.wait_ge(id0, 3)
            nc.gpsimd.memset(ident[:, :], 0.0).then_inc(zeroed, 1)
            pool.wait_ge(zeroed, EARLY_POOL)
            nc.gpsimd.affine_select(out=ident[:, :], in_=ident[:, :], compare_op=ALU.not_equal, fill=1.0,
                                    base=0, pattern=[[-1, 128]], channel_multiplier=1).then_inc(const, 1)
            nc.gpsimd.iota(iota_i[:, :], pattern=[[1, WIN]], base=0, channel_multiplier=0).then_inc(const, 1)
            for g in range(4):
                pool.wait_ge(const, 2 + g)
                nc.gpsimd.iota(rel_i[32 * g:32 * g + 32, :], pattern=[[1, 1]], base=0,
                               channel_multiplier=1).then_inc(const, 1)
            pool.wait_ge(const, 6)
            nc.gpsimd.memset(ones[:, :], 1.0).then_inc(const, 1)
            nc.gpsimd.memset(lin2[:, :, :], 0.0).then_inc(const, 1)
            for b in range(BASES):
                nc.gpsimd.memset(acc[:, b, :], 0.0).then_inc(acc0_zero, 1)

            def gather_pass(p, table, r):
                def gather(i, s, m):
                    pool.wait_ge(p.idx_ready, chunks_done(i, r))
                    pool.sem_inc(gather_turn, 1)
                    for t in range(TILES):
                        pool.indirect_dma_start(
                            out=got[:, s, t, :], out_offset=None, in_=table,
                            in_offset=bass.IndirectOffsetOnAxis(ap=idx_c[:, s, t:t + 1], axis=0),
                        ).then_inc(p.gathered[s], 16)

                pairs(pool, gather, gather, gather)

            def both_paths(p, table):
                gather_pass(p, table, 0)
                many = pool.value_load(general[0:1, 0:1], min_val=0, max_val=1)
                with pool.If(many > 0):
                    with pool.Fori(1, WINDOWS) as r:
                        gather_pass(p, table, r)

            pool.wait_ge(t0_out[0], 16 * 3)
            pool.wait_ge(t0_out[1], 16 * 2)
            both_paths(p0, table0)

            for g in range(GROUPS):
                pool.wait_ge(l0_mm, (g + 1) * GB)
                n1 = (g + 1) * GB * NB if g < GROUPS - 1 else ACC_N
                nc.gpsimd.memset(acc[:, :, g * GB * NB:n1], 0.0).then_inc(acc1_zero, 1)
            pool.wait_ge(t1_out[0], 16 * 3)
            pool.wait_ge(t1_out[1], 16 * 2)
            both_paths(p1, table1)

        @block.scalar
        def _(act):
            act.wait_ge(vared, 1)
            nc.scalar.activation(std[:, :], var_eps[:, :], ACT.Sqrt).then_inc(rooted, 1)
            act.wait_ge(nmred, 1)
            for g in range(GROUPS):
                if g >= 2:
                    act.wait_ge(tp_done, (g - 1) * GB)
                for j in range(GB):
                    b = g * GB + j
                    nc.scalar.activation(hn[:, g % 2, j, :], xs[:, b, :], ACT.Relu, bias=nmr[:, b:b + 1],
                                         scale=rstd[:, b:b + 1]).then_inc(normed, 1)

            act.wait_ge(const, 8)
            act.wait_ge(w_in, 16 * N_WEIGHTS)

            def place(q, part, comp, stage, scale):
                rows_ = slice(MUL * part, MUL * (part + 1))
                dst_ = lin2[rows_, q, 0:MUL] if comp is None else lin2[rows_, q, MUL + comp:FEAT:3]
                nc.scalar.activation(dst_, stage[rows_, :], ACT.Copy, scale=scale).then_inc(lin2_ready, 1)

            place(0, 0, None, lin2_a, LIN2_SCALE)
            place(0, 2, 2, lin2_a, LIN2_SCALE)
            for i in range(3):
                place(1 + i, 1, i, lin2_a, LIN2_SCALE)
            place(3, 3, None, lin2_a, LIN2_SCALE * INV_SQRT3)
            place(4, 0, 0, lin2_b, LIN2_SCALE)
            place(4, 2, 1, lin2_b, LIN2_SCALE)
            place(5, 1, None, lin2_b, LIN2_SCALE * INV_SQRT3)
            place(6, 3, None, lin2_b, LIN2_SCALE * INV_SQRT3)

            def take_list(p, i, s):
                nc.scalar.activation(idx_c[:, s, :], src_t[:, bass.ds(i, 1), :].rearrange("p a t -> p (a t)"),
                                     ACT.Copy).then_inc(p.idx_ready, 1)

            def hidden(i, s, r):
                act.wait_ge(xT_done, chunks_done(i, r))
                nc.scalar.activation(xT[:, s, :], psum[0:TILES * 8, 0, s * 128:(s + 1) * 128],
                                     ACT.Copy).then_inc(xT_copied, 1)
                act.wait_ge(hid_done, chunks_done(i, r))
                nc.scalar.activation(hid[:, s, :, :], psum[:, 1, :].rearrange("p (v e) -> p v e", e=128),
                                     ACT.Silu, scale=FC1_SCALE).then_inc(silu_done, 1)

            def edge_pass0(r):
                take_list(p0, 0, 0)
                take_list(p0, 1, 1)
                hidden(0, 0, r)

                def step(i, s, m):
                    hidden(i + 1, 1 - s, r)
                    act.wait_ge(p0.gathered[s], 16 * TILES * slot_uses(s, m, r))
                    act.wait_ge(prod_done, chunks_done(i, r))
                    take_list(p0, i + 2, s)

                def tail():
                    hidden(LAST, 0, r)

                step(0, 0, 0)
                step(1, 1, 0)
                with act.Fori(1, PAIRS - 1) as m:
                    for s in range(2):
                        step(m * 2 + s, s, m)
                step(LAST - 2, 0, PAIRS - 1)
                tail()

            act.wait_ge(tables, 1)
            edge_pass0(0)
            many = act.value_load(general[0:1, 0:1], min_val=0, max_val=1)
            with act.If(many > 0):
                with act.Fori(1, WINDOWS) as r:
                    act.wait_ge(tables, r + 1)
                    edge_pass0(r)

            for g in range(GROUPS):
                act.wait_ge(n1_var, g + 1)
                nc.scalar.activation(std[:, g * GB:(g + 1) * GB], var_eps[:, g * GB:(g + 1) * GB],
                                     ACT.Sqrt).then_inc(n1_root, 1)
                act.wait_ge(n1_nmr, g + 1)
                if g >= 2:
                    act.wait_ge(t1_out[g % 2], 16 * (g // 2))
                for j in range(GB):
                    b = g * GB + j
                    nc.scalar.activation(hn[:, g % 2, j, :], xs[:, b, :], ACT.Relu, bias=nmr[:, b:b + 1],
                                         scale=rstd[:, b:b + 1]).then_inc(n1_normed, 1)

            def select(i, s):
                nc.scalar.activation(sel_c[:, s, :], ident_bf[0:CHUNKS, bass.ds(i, 1)].to_broadcast([CHUNKS, 32]),
                                     ACT.Copy).then_inc(sel_ready, 1)

            def edge_pass1(r):
                for s in range(2):
                    take_list(p1, s, s)
                    select(s, s)

                def step(i, s, m):
                    act.wait_ge(typ_done, chunks_done(i, r))
                    select(i + 2, s)
                    act.wait_ge(p1.gathered[s], 16 * TILES * slot_uses(s, m, r))
                    act.wait_ge(p1.agg_done, chunks_done(i, r))
                    take_list(p1, i + 2, s)

                step(0, 0, 0)
                step(1, 1, 0)
                with act.Fori(1, PAIRS - 1) as m:
                    for s in range(2):
                        step(m * 2 + s, s, m)
                step(LAST - 2, 0, PAIRS - 1)

            edge_pass1(0)
            many = act.value_load(general[0:1, 0:1], min_val=0, max_val=1)
            with act.If(many > 0):
                with act.Fori(1, WINDOWS) as r:
                    act.wait_ge(tables1, r)
                    edge_pass1(r)

        @block.vector
        def _(dve):
            for g in range(GROUPS):
                dve.wait_ge(x_in[g], 16)
                if g:
                    dve.wait_ge(aggr, g * GB)
                for j in range(GB):
                    nc.vector.bn_stats(stats[:, j, :], xs[:, g * GB + j, :]).then_inc(stat, 1)
                for j in range(GB):
                    dve.wait_ge(stat, g * GB + j + 1)
                    nc.vector.bn_aggr(mv[:, g * GB + j, :], stats[:, j, :]).then_inc(aggr, 1)
            dve.wait_ge(aggr, BLOCKS)
            nc.vector.tensor_scalar_add(var_eps[:, :], mv[:, :, 1], EPS).then_inc(vared, 1)
            dve.wait_ge(rooted, 1)
            nc.vector.reciprocal(rstd[:, :], std[:, :]).then_inc(inv, 1)
            dve.wait_ge(inv, 1)
            nc.vector.scalar_tensor_tensor(out=nmr[:, :], in0=mv[:, :, 0], scalar=-1.0, in1=rstd[:, :],
                                           op0=ALU.mult, op1=ALU.mult).then_inc(nmred, 1)

            dve.wait_ge(const, 8)
            nc.vector.tensor_copy(iota_w[:, :], iota_i[:, :]).then_inc(consts_f, 1)
            nc.vector.tensor_copy(rel_id[:, :], rel_i[:, :]).then_inc(consts_f, 1)
            nc.vector.tensor_copy(ident_bf[:, :], ident[:, :]).then_inc(consts_f, 1)

            dve.wait_ge(e_in, 16 * 8)
            nc.vector.tensor_copy(src_f, src_i).then_inc(d_rows, 1)
            nc.vector.tensor_copy(et_rows[:, :], et_i).then_inc(d_rows, 1)
            nc.vector.tensor_copy(dst_f, dst_i).then_inc(d_step, 1)
            dve.wait_ge(d_step, 1)
            halves = dst_f.rearrange("c (h e) -> c h e", h=H)
            nc.vector.tensor_reduce(dmax[:, :], halves, AX.X, ALU.max).then_inc(d_step, 1)
            nc.vector.tensor_scalar(dst_hi, dst_f, 0.0, PAD_HIGH, ALU.is_lt, ALU.mult).then_inc(d_step, 1)
            dve.wait_ge(d_step, 3)
            nc.vector.tensor_tensor(dst_hi, dst_hi, dst_f, ALU.add).then_inc(d_step, 1)
            dve.wait_ge(d_step, 4)
            nc.vector.tensor_reduce(dmin[:, :], dst_hi.rearrange("c (h e) -> c h e", h=H), AX.X,
                                    ALU.min).then_inc(d_step, 1)
            dve.wait_ge(d_step, 5)
            nc.vector.tensor_tensor(span[:, :], dmax[:, :], dmin[:, :], ALU.subtract).then_inc(d_step, 1)
            dve.wait_ge(d_step, 6)
            nc.vector.tensor_scalar(wide[:, :], span[:, :], float(WIN), None, ALU.is_ge).then_inc(d_step, 1)
            dve.wait_ge(d_step, 7)
            nc.vector.tensor_reduce(nwide[:, :], wide[:, :], AX.X, ALU.add).then_inc(d_step, 1)
            dve.wait_ge(cnt_done, 1)
            nc.vector.tensor_scalar(narrow[:, :], psum[:, 7, 0:1], 0.5, None, ALU.is_lt).then_inc(d_step, 1)
            nc.vector.tensor_scalar(general[:, :], psum[0:1, 7, 0:1], 0.5, None, ALU.is_gt).then_inc(d_step, 1)
            dve.wait_ge(d_step, 10)
            nc.vector.tensor_scalar(dmin[:, :], dmin[:, :], narrow[0:CHUNKS, :], None, ALU.mult).then_inc(d_step, 1)
            dve.wait_ge(d_step, 11)
            for h in range(H):
                nc.vector.tensor_scalar(dst_hi[:, h * HALF:(h + 1) * HALF], dst_f[:, h * HALF:(h + 1) * HALF],
                                        dmin[:, h:h + 1], None, ALU.subtract).then_inc(d_rows, 1)

            def copy_hT(g):
                dve.wait_ge(tp_done, (g + 1) * GB)
                if g >= 2:
                    dve.wait_ge(t0_mm, (g - 1) * GB)
                for a, n in IN_BANKS:
                    nc.vector.tensor_copy(hT[:, g % 2, a:a + n, :],
                                          in_bank(a // 3, n)[:, :, 0:NB]).then_inc(hT_copied, 1)

            def copy_t0(g):
                dve.wait_ge(t0_mm, (g + 1) * GB)
                if g >= 2:
                    dve.wait_ge(t0_out[g % 2], 16 * (g // 2))
                for a, n in IN_BANKS:
                    nc.vector.tensor_copy(rows_out[:, g % 2, a:a + n, :],
                                          in_bank(2 + a // 3, n)[0:NB, :, :]).then_inc(t0_rows, 1)

            copy_hT(0)
            for g in range(1, GROUPS):
                copy_hT(g)
                copy_t0(g - 1)
            copy_t0(GROUPS - 1)

            for n, tab in enumerate((src_t, rel_t, ew_t)):
                for h in range(H):
                    dve.wait_ge(tr_done, K * (H * n + h + 1))
                    nc.vector.tensor_copy(
                        tab[:, :, K * h:K * (h + 1)].rearrange("p c k -> p k c"),
                        psum[:, 5 + h, 0:K * CHUNKS].rearrange("p (k c) -> p k c", k=K)).then_inc(tr_copied, 1)
            dve.wait_ge(min_done, 2)
            for h in range(H):
                nc.vector.tensor_copy(wmin_f[:, :, h], psum[0:1, 7, 128 * (h + 1):128 * (h + 1) + CHUNKS])\
                    .then_inc(d_step, 1)
            dve.wait_ge(d_step, 13)
            nc.vector.tensor_copy(wmin[:, :, :], wmin_f[:, :, :]).then_inc(d_step, 1)
            dve.wait_ge(d_step, 14)
            dve.wait_ge(tr_copied, 6)
            dve.wait_ge(acc0_zero, BASES)
            nc.vector.tensor_scalar_add(narrow[0:1, :], narrow[0:1, :], 0.0).then_inc(tables, 1)

            def one_hot(p, i, s, r):
                rel = rel_t[:, bass.ds(i, 1), :].rearrange("p a t -> p (a t)").unsqueeze(2)
                nc.vector.tensor_tensor(onehot[:, s, :, :], rel.broadcast_to([128, TILES, WIN]),
                                        iota_w[:, :].unsqueeze(1).broadcast_to([128, TILES, WIN]),
                                        ALU.is_equal).then_inc(p.onehot, 1)

            def spread(p, coefs, n, s, i, r):
                dve.wait_ge(p.onehot, chunks_done(i, r))
                o = oc[:, s, 0:TILES * n * WIN].rearrange("p (t n w) -> p t n w", t=TILES, n=n)
                nc.vector.tensor_tensor(o, coefs.unsqueeze(3).broadcast_to([128, TILES, n, WIN]),
                                        onehot[:, s, :, :].unsqueeze(2).broadcast_to([128, TILES, n, WIN]),
                                        ALU.mult).then_inc(p.oc_done, 1)

            def accumulate(p, n, i, s, r, first):
                starts = [dve.value_load(wmin[0:1, bass.ds(i, 1), h:h + 1].rearrange("p a b -> p (a b)"),
                                         min_val=0, max_val=NODES - 1) for h in range(H)]
                dve.wait_ge(p.agg_done, chunks_done(i, r))
                for h in range(H):
                    if not (first and h == 0):
                        dve.wait_ge(p.acc_done, (r * CHUNKS + i) * H + h)
                    window = acc[:, 0:n, bass.ds(starts[h], WIN)]
                    sums = psum[:, 6 + s, h * n * WIN:(h + 1) * n * WIN].rearrange("p (n w) -> p n w", n=n)
                    nc.vector.tensor_tensor(window, window, sums, ALU.add).then_inc(p.acc_done, 1)

            def edges0(i, s, m, r, loads=1):
                one_hot(p0, i, s, r)
                dve.wait_ge(ea4_in[s], ea_loads(s, m, r, loads))
                spread(p0, ea4_c[:, s, :, :].rearrange("p h (k c) -> p (h k) c", c=COEF), COEF, s, i, r)
                dve.wait_ge(w_done, chunks_done(i, r))
                dve.wait_ge(p0.gathered[s], 16 * TILES * slot_uses(s, m, r))
                w = psum[:, 2 + 2 * s:4 + 2 * s, :].rearrange("p b (t f) -> p (b t) f", f=128)
                w = w.rearrange("p t (j u) -> p t j u", u=MUL)
                for n, (j, part, to) in enumerate(((0, 0, 0), (2, 3, 64), (2, 1, 128), (2, 2, 192))):
                    o = prod[:, s, :, to:to + 64].rearrange("p t (j u) -> p t j u", u=MUL)
                    v = got[:, s, :, MUL * part:MUL * (part + 1)].unsqueeze(2).broadcast_to([128, TILES, 2, MUL])
                    last = nc.vector.tensor_tensor(o, w[:, :, j:j + 2, :], v, ALU.mult)
                last.then_inc(prod_done, 1)

            def edge_pass0(r, first=False):
                def start0(i, s, m):
                    edges0(i, s, m, r)

                edges0(0, 0, 0, r)
                edges0(1, 1, 0, r)
                accumulate(p0, Q, 0, 0, r, first)
                with dve.Fori(1, PAIRS) as m:
                    for s in range(2):
                        edges0(m * 2 + s, s, m, r)
                        accumulate(p0, Q, m * 2 + s - 1, 1 - s, r, False)
                edges0(LAST, 0, PAIRS, r, 3)
                accumulate(p0, Q, LAST - 1, 1, r, False)
                accumulate(p0, Q, LAST, 0, r, False)
                dve.wait_ge(p0.acc_done, H * chunks_done(LAST, r))

            def shift_windows(by, done):
                nc.vector.tensor_scalar_add(rel_t[:, :, :], rel_t[:, :, :], float(-by)).then_inc(shifted, 1)
                nc.vector.tensor_scalar_add(wmin_f[:, :, :], wmin_f[:, :, :], float(by)).then_inc(shifted, 1)

            edge_pass0(0, True)
            many = dve.value_load(general[0:1, 0:1], min_val=0, max_val=1)
            with dve.If(many > 0):
                with dve.Fori(1, WINDOWS) as r:
                    shift_windows(WIN, None)
                    dve.wait_ge(shifted, r * 3 - 1)
                    nc.vector.tensor_copy(wmin[:, :, :], wmin_f[:, :, :]).then_inc(shifted, 1)
                    dve.wait_ge(shifted, r * 3)
                    nc.vector.tensor_scalar_add(narrow[0:1, :], narrow[0:1, :], 0.0).then_inc(tables, 1)
                    edge_pass0(r)

            for g in range(GROUPS):
                for j in range(GB):
                    b = g * GB + j
                    dve.wait_ge(l0_mm, b + 1)
                    nc.vector.tensor_tensor(xs[:, b, :], psum[0:NB, j, 0:FEAT], xs[:, b, :],
                                            ALU.add).then_inc(l0_add, 1)
                for j in range(GB):
                    b = g * GB + j
                    dve.wait_ge(l0_add, b + 1)
                    nc.vector.bn_stats(stats[:, j, :], xs[:, b, :]).then_inc(n1_stat, 1)
                for j in range(GB):
                    b = g * GB + j
                    dve.wait_ge(n1_stat, b + 1)
                    nc.vector.bn_aggr(mv[:, b, :], stats[:, j, :]).then_inc(n1_aggr, 1)
                bl = slice(g * GB, (g + 1) * GB)
                dve.wait_ge(n1_aggr, (g + 1) * GB)
                nc.vector.tensor_scalar_add(var_eps[:, bl], mv[:, bl, 1], EPS).then_inc(n1_var, 1)
                dve.wait_ge(n1_root, g + 1)
                nc.vector.reciprocal(rstd[:, bl], std[:, bl]).then_inc(n1_inv, 1)
                dve.wait_ge(n1_inv, g + 1)
                nc.vector.scalar_tensor_tensor(out=nmr[:, bl], in0=mv[:, bl, 0], scalar=-1.0, in1=rstd[:, bl],
                                               op0=ALU.mult, op1=ALU.mult).then_inc(n1_nmr, 1)

            def type_rows(i, s, r):
                dve.wait_ge(typ_done, chunks_done(i, r))
                nc.vector.tensor_scalar(typ1[:, s, :], psum[:, 2 * s, 0:H * 128], rel_id[:, :], None,
                                        ALU.is_equal).then_inc(typ1_done, 1)

            def edges1(i, s, m, r):
                one_hot(p1, i, s, r)
                dve.wait_ge(cf_done, chunks_done(i, r))
                cf = psum[:, 1 + 2 * s, 0:TILES * BASES].rearrange("p (t b) -> p t b", b=BASES)
                ew = ew_t[:, bass.ds(i, 1), :].rearrange("p a t -> p (a t)").unsqueeze(2)
                nc.vector.tensor_tensor(coef[:, s, :, :], cf, ew.broadcast_to([128, TILES, BASES]),
                                        ALU.mult).then_inc(coef_done, 1)
                dve.wait_ge(coef_done, chunks_done(i, r))
                spread(p1, coef[:, s, :, :], BASES, s, i, r)

            def edge_pass1(r, first=False):
                type_rows(0, 0, r)
                edges1(0, 0, 0, r)
                type_rows(1, 1, r)
                edges1(1, 1, 0, r)
                type_rows(2, 0, r)
                accumulate(p1, BASES, 0, 0, r, first)
                with dve.Fori(1, PAIRS) as m:
                    for s in range(2):
                        edges1(m * 2 + s, s, m, r)
                        if s == 0:
                            type_rows(m * 2 + 1, 1, r)
                        else:
                            type_rows(m * 2 + 2, 0, r)
                        accumulate(p1, BASES, m * 2 + s - 1, 1 - s, r, False)
                edges1(LAST, 0, PAIRS, r)
                accumulate(p1, BASES, LAST - 1, 1, r, False)
                accumulate(p1, BASES, LAST, 0, r, False)
                dve.wait_ge(p1.acc_done, H * chunks_done(LAST, r))

            dve.wait_ge(acc1_zero, GROUPS)
            edge_pass1(0, True)
            many = dve.value_load(general[0:1, 0:1], min_val=0, max_val=1)
            with dve.If(many > 0):
                with dve.Fori(1, WINDOWS) as r:
                    shift_windows(-WIN, None)
                    dve.wait_ge(shifted, 3 * (WINDOWS - 1) + r * 3 - 1)
                    nc.vector.tensor_copy(wmin[:, :, :], wmin_f[:, :, :]).then_inc(shifted, 1)
                    dve.wait_ge(shifted, 3 * (WINDOWS - 1) + r * 3)
                    nc.vector.tensor_scalar_add(narrow[0:1, :], narrow[0:1, :], 0.0).then_inc(tables1, 1)
                    edge_pass1(r)

            for g in range(GROUPS):
                if g >= 2:
                    dve.wait_ge(y_out[g % 2], 16 * (g // 2))
                for j in range(GB):
                    b = g * GB + j
                    dve.wait_ge(l1_mm, b + 1)
                    if b >= GB:
                        dve.wait_ge(l1_rows, b - GB + 1)
                    y = ybias[:, j, :]
                    nc.vector.tensor_tensor(y, psum[0:NB, j, 0:FEAT], bias_b[:, :], ALU.add).then_inc(l1_bias, 1)
                for j in range(GB):
                    b = g * GB + j
                    dve.wait_ge(l1_bias, b + 1)
                    nc.vector.scalar_tensor_tensor(out=rows_out[:, g % 2, j, :], in0=ybias[:, j, :], scalar=0.0,
                                                   in1=xs[:, b, :], op0=ALU.max, op1=ALU.add).then_inc(l1_rows, 1)

        @block.tensor
        def _(pe):
            pe.wait_ge(const, 1)

            def transpose_group(g):
                pe.wait_ge(normed, (g + 1) * GB)
                if g:
                    pe.wait_ge(hT_copied, 2 * g)
                for j in range(GB):
                    nc.tensor.transpose(in_bank(j // 3, 3)[:, j % 3, 0:NB], hn[:, g % 2, j, :],
                                        ident[0:NB, 0:NB]).then_inc(tp_done, 1)

            def lin1_group(g):
                pe.wait_ge(hT_copied, 2 * (g + 1))
                if g:
                    pe.wait_ge(t0_rows, 2 * g)
                for j in range(GB):
                    nc.tensor.matmul(in_bank(2 + j // 3, 3)[0:NB, j % 3, :], hT[:, g % 2, j, :], lin1[:, :],
                                     start=True, stop=True).then_inc(t0_mm, 1)

            def count_wide():
                pe.wait_ge(d_step, 8)
                nc.tensor.matmul(psum[:, 7, 0:1], ones[0:CHUNKS, :], nwide[:, :], start=True, stop=True)\
                    .then_inc(cnt_done, 1)

            pe.wait_ge(const, 8)
            transpose_group(0)
            pe.wait_ge(lin1_in, 16 * 4)
            count_wide()
            for g in range(1, GROUPS):
                transpose_group(g)
                lin1_group(g - 1)
            lin1_group(GROUPS - 1)

            pe.wait_ge(d_rows, 4)
            for n, row in enumerate((src_f, dst_hi, ew_f)):
                for h in range(H):
                    if n:
                        pe.wait_ge(tr_copied, H * (n - 1) + h + 1)
                    for k in range(K):
                        nc.tensor.transpose(psum[:, 5 + h, k * CHUNKS:(k + 1) * CHUNKS],
                                            row[:, h * HALF + k:(h + 1) * HALF:K],
                                            ident[0:CHUNKS, 0:CHUNKS]).then_inc(tr_done, 1)
            for h in range(H):
                nc.tensor.transpose(psum[0:1, 7, 128 * (h + 1):128 * (h + 1) + CHUNKS], dmin[:, h:h + 1],
                                    ident[0:CHUNKS, 0:CHUNKS]).then_inc(min_done, 1)

            def turn_attributes(i, s, m, r, loads=1):
                pe.wait_ge(ea8_in[s], ea_loads(s, m, r, loads))
                pe.sem_inc(turn_turn, 1)
                nc.tensor.transpose(psum[0:TILES * 8, 0, s * 128:(s + 1) * 128],
                                    ea8_c[:, s, :, :].rearrange("p h c -> p (h c)"), ident[:, :]).then_inc(xT_done, 1)

            def hidden(i, s, r):
                pe.wait_ge(xT_copied, chunks_done(i, r))
                for v in range(TILES // 2):
                    last = nc.tensor.matmul(psum[:, 1, v * 128:(v + 1) * 128], fc1_bd[:, v, :], xT[:, s, :],
                                            start=True, stop=True)
                last.then_inc(hid_done, 1)

            def edge_weights(i, s, r, free):
                pe.wait_ge(silu_done, chunks_done(i, r))
                if free:
                    pe.wait_ge(prod_done, chunks_done(i - 2, r))
                for v in range(TILES // 2):
                    last = nc.tensor.matmul(psum[:, 2 + 2 * s + v // 2, (v % 2) * 256:(v % 2 + 1) * 256],
                                            hid[:, s, v, :], fc2_bd[:, :], start=True, stop=True)
                last.then_inc(w_done, 1)

            def sums0(i, s, r, free):
                pe.wait_ge(prod_done, chunks_done(i, r))
                pe.wait_ge(p0.oc_done, chunks_done(i, r))
                if free:
                    pe.wait_ge(p0.acc_done, H * chunks_done(i - 2, r))
                for h in range(H):
                    for a, q0, qn in ((0, 0, QA), (128, QA, QB)):
                        o = (h * Q + q0) * WIN
                        for k in range(K):
                            t = h * K + k
                            c = t * COEF * WIN
                            last = nc.tensor.matmul(psum[:, 6 + s, o:o + qn * WIN], prod[:, s, t, a:a + 128],
                                                    oc[:, s, c:c + qn * WIN], start=(k == 0), stop=(k == K - 1))
                last.then_inc(p0.agg_done, 1)

            def edge_pass0(r):
                turn_attributes(0, 0, 0, r)
                hidden(0, 0, r)
                turn_attributes(1, 1, 0, r)
                edge_weights(0, 0, r, False)
                hidden(1, 1, r)
                turn_attributes(2, 0, 1, r)
                edge_weights(1, 1, r, False)
                hidden(2, 0, r)
                sums0(0, 0, r, False)
                turn_attributes(3, 1, 1, r)
                edge_weights(2, 0, r, True)
                hidden(3, 1, r)
                sums0(1, 1, r, False)
                turn_attributes(4, 0, 2, r)
                edge_weights(3, 1, r, True)
                hidden(4, 0, r)
                sums0(2, 0, r, True)
                with pe.Fori(2, PAIRS - 1) as m:
                    turn_attributes(m * 2 + 1, 1, m, r)
                    edge_weights(m * 2, 0, r, True)
                    hidden(m * 2 + 1, 1, r)
                    sums0(m * 2 - 1, 1, r, True)
                    turn_attributes(m * 2 + 2, 0, m + 1, r)
                    edge_weights(m * 2 + 1, 1, r, True)
                    hidden(m * 2 + 2, 0, r)
                    sums0(m * 2, 0, r, True)
                m = PAIRS - 1
                turn_attributes(m * 2 + 1, 1, m, r)
                edge_weights(m * 2, 0, r, True)
                hidden(m * 2 + 1, 1, r)
                sums0(m * 2 - 1, 1, r, True)
                turn_attributes(LAST, 0, PAIRS, r, 3)
                edge_weights(m * 2 + 1, 1, r, True)
                hidden(LAST, 0, r)
                sums0(m * 2, 0, r, True)
                edge_weights(LAST, 0, r, True)
                sums0(LAST - 1, 1, r, True)
                sums0(LAST, 0, r, True)

            pe.wait_ge(w_in, 16 * N_WEIGHTS)
            pe.wait_ge(tables, 1)
            edge_pass0(0)
            many = pe.value_load(general[0:1, 0:1], min_val=0, max_val=1)
            with pe.If(many > 0):
                with pe.Fori(1, WINDOWS) as r:
                    pe.wait_ge(tables, r + 1)
                    edge_pass0(r)

            pe.wait_ge(lin2_ready, 10)
            pe.wait_ge(p0.acc_done, H * CHUNKS)

            def node_block(b, n, w, done):
                for q in range(n):
                    last = nc.tensor.matmul(psum[0:NB, b % GB, 0:FEAT], acc[:, q, b * NB:(b + 1) * NB], w[:, q, :],
                                            start=(q == 0), stop=(q == n - 1))
                last.then_inc(done, 1)

            for b in range(BLOCKS):
                if b >= GB:
                    pe.wait_ge(l0_add, b - GB + 1)
                node_block(b, Q, lin2, l0_mm)

            def spread_types(i, s, r):
                pe.wait_ge(sel_ready, chunks_done(i, r))
                for k in range(K):
                    last = nc.tensor.matmul(psum[32 * k:32 * k + 32, 2 * s, 0:H * 128], sel_c[:, s, :],
                                            et_rows[:, k:CHUNK:K], start=True, stop=True)
                last.then_inc(typ_done, 1)

            def coefficients(i, s, r):
                pe.wait_ge(typ1_done, chunks_done(i, r))
                for h in range(H):
                    last = nc.tensor.matmul(psum[:, 1 + 2 * s, 32 * h:32 * (h + 1)],
                                            typ1[:, s, 128 * h:128 * (h + 1)], wc_bd[:, :], start=True, stop=True)
                last.then_inc(cf_done, 1)

            def sums1(i, s, m, r, free):
                pe.wait_ge(p1.gathered[s], 16 * TILES * slot_uses(s, m, r))
                pe.wait_ge(p1.oc_done, chunks_done(i, r))
                if free:
                    pe.wait_ge(p1.acc_done, H * chunks_done(i - 2, r))
                n = BASES * WIN
                for h in range(H):
                    for k in range(K):
                        t = h * K + k
                        last = nc.tensor.matmul(psum[:, 6 + s, h * n:(h + 1) * n], got[:, s, t, :],
                                                oc[:, s, t * n:(t + 1) * n], start=(k == 0), stop=(k == K - 1))
                last.then_inc(p1.agg_done, 1)

            def edge_pass1(r):
                spread_types(0, 0, r)
                spread_types(1, 1, r)
                coefficients(0, 0, r)
                spread_types(2, 0, r)
                coefficients(1, 1, r)
                sums1(0, 0, 0, r, False)
                spread_types(3, 1, r)
                coefficients(2, 0, r)
                sums1(1, 1, 0, r, False)
                spread_types(4, 0, r)
                coefficients(3, 1, r)
                sums1(2, 0, 1, r, True)
                with pe.Fori(2, PAIRS) as m:
                    spread_types(m * 2 + 1, 1, r)
                    coefficients(m * 2, 0, r)
                    sums1(m * 2 - 1, 1, m - 1, r, True)
                    spread_types(m * 2 + 2, 0, r)
                    coefficients(m * 2 + 1, 1, r)
                    sums1(m * 2, 0, m, r, True)
                coefficients(LAST, 0, r)
                sums1(LAST - 1, 1, PAIRS - 1, r, True)
                sums1(LAST, 0, PAIRS, r, True)

            edge_pass1(0)
            many = pe.value_load(general[0:1, 0:1], min_val=0, max_val=1)
            with pe.If(many > 0):
                with pe.Fori(1, WINDOWS) as r:
                    pe.wait_ge(tables1, r)
                    edge_pass1(r)

            pe.wait_ge(p1.acc_done, H * CHUNKS)
            for b in range(BLOCKS):
                if b >= GB:
                    pe.wait_ge(l1_bias, b - GB + 1)
                node_block(b, BASES, w_base, l1_mm)


_INS = ["x", "src", "dst", "edge_attr_4", "edge_attr_8", "edge_type_32", "edge_weight1", "L0_gnn_w_lin1_s",
        "L0_gnn_w_lin1_v", "L0_gnn_fc_w1", "L0_gnn_fc_w2", "L0_gnn_w_lin2_s", "L0_gnn_w_lin2_v",
        "L1_gnn_weight", "L1_gnn_w_comp", "L1_gnn_bias_param"]


def kernel(**inputs):
    import numpy as _np
    import concourse.bacc as _bacc
    from concourse.bass_utils import run_bass_kernel_spmd as _run

    nc = _bacc.Bacc("TRN2", target_bir_lowering=False, num_devices=1)
    arrays, args = {}, []
    for name in _INS:
        a = _np.ascontiguousarray(inputs[name])
        if name == "edge_weight1":
            a = a.reshape(-1)
        arrays[f"in_{name}"] = a
        args.append(nc.dram_tensor(f"in_{name}", a.shape, mybir.dt.from_np(a.dtype), kind="ExternalInput").ap())
    for name in ("table0", "table1"):
        args.append(nc.dram_tensor(name, [NODES, FEAT], FP32, kind="Internal").ap())
    args.append(nc.dram_tensor("out_0", [NODES, FEAT], FP32, kind="ExternalOutput").ap())
    gnn_two_layers(nc, *args)
    r = _run(nc, [arrays], core_ids=[0])
    return r.results[0]["out_0"]
```

```python
import concourse.bass as bass
from concourse import mybir
from contextlib import ExitStack

FP32 = mybir.dt.float32
BF16 = mybir.dt.bfloat16
FP16 = mybir.dt.float16
I32 = mybir.dt.int32
ALU = mybir.AluOpType
ACT = mybir.ActivationFunctionType
AX = mybir.AxisListType

NODES = 3125
FEAT = 128
EDGES = 103125
MUL = 32
HID = 64
BASES = 8
RELS = 32

NB = 125
BLOCKS = NODES // NB
GB = 5
GROUPS = BLOCKS // GB

WIN = 24
HALF = 512
K = HALF // 128
H = 2
TILES = H * K
CHUNK = H * HALF
CHUNKS = -(-EDGES // CHUNK)
TAIL = EDGES - (CHUNKS - 1) * CHUNK
TAIL1 = TAIL - HALF
LAST = CHUNKS - 1
PAIRS = CHUNKS // 2
assert HALF < TAIL < CHUNK and CHUNKS % 2 == 1 and CHUNKS <= 128
WINDOWS = -(-NODES // WIN)
ACC_N = NODES + WIN - 1

COEF = 4
QA = 4
QB = 3
Q = QA + QB

PICK_T = TILES - 1
PICK_SCALE = 4096.0
MID_NODE = NODES // 2
PICK_HALVES = ((0, 13), (13, BLOCKS))
assert PICK_SCALE * FEAT ** 0.5 < 65504 and MID_NODE < 2048
GOT = 4
QUADS = CHUNKS // GOT

EPS = 1e-5
SILU_NORM = 1.6791767923989418
NUM_NEIGHBORS = 16.0
FC1_SCALE = 8 ** -0.5
LIN2_SCALE = MUL ** -0.5 * SILU_NORM * HID ** -0.5 * NUM_NEIGHBORS ** -0.5 * (2 * MUL) ** -0.5
INV_SQRT3 = 3.0 ** -0.5
PAD_LOW = -1.0
PAD_HIGH = 8192.0


def gnn_two_layers(nc, x, src, dst, ea4, ea8, etype, eweight, lin1_s, lin1_v, fc1, fc2, lin2_s, lin2_v,
                   weight, w_comp, bias, table0, table1, src_row, out):
    ctx = ExitStack()
    with ctx:
        def sb(name, shape, dt):
            return ctx.enter_context(nc.sbuf_tensor(name, shape, dt))

        def sem(name):
            return ctx.enter_context(nc.semaphore(name))

        ident = sb("ident", [128, 128], FP32)
        ident_bf = sb("ident_bf", [128, 128], BF16)
        iota_i = sb("iota_i", [128, WIN], I32)
        iota_w = sb("iota_w", [128, WIN], FP32)
        rel_i = sb("rel_i", [128, 1], I32)
        rel_id = sb("rel_id", [128, 1], FP32)
        ones = sb("ones", [128, 128], FP32)

        lin1 = sb("lin1", [FEAT, FEAT], FP32)
        fc1_bd = sb("fc1_bd", [TILES * 8, TILES // 2, 128], FP32)
        fc2_bd = sb("fc2_bd", [128, 256], FP32)
        lin2_a = sb("lin2_a", [128, MUL], FP32)
        lin2_b = sb("lin2_b", [128, MUL], FP32)
        lin2 = sb("lin2", [128, Q, FEAT], FP32)
        wc_bd = sb("wc_bd", [128, K * BASES], FP32)
        w_base = sb("w_base", [FEAT, BASES, FEAT], FP32)
        bias_c = sb("bias_c", [FEAT, 1], FP32)

        xs = sb("xs", [NB, BLOCKS, FEAT], FP32)
        stats = sb("stats", [NB, GB, 6], FP32)
        mv = sb("mv", [NB, BLOCKS, 2], FP32)
        var_eps = sb("var_eps", [NB, BLOCKS], FP32)
        std = sb("std", [NB, BLOCKS], FP32)
        rstd = sb("rstd", [NB, BLOCKS], FP32)
        nmr = sb("nmr", [NB, BLOCKS], FP32)
        hn = sb("hn", [NB, 2, GB, FEAT], FP32)
        hT = sb("hT", [FEAT, 2, GB, NB], FP32)
        rows_out = sb("rows_out", [NB, 2, GB, FEAT], FP32)
        acc = [sb(f"acc{n}", [FEAT, ACC_N], FP32) for n in range(2)]
        acc_y = sb("acc_y", [FEAT, NODES], FP32)

        table_16 = sb("table_16", [NB, BLOCKS, 2, FEAT], FP16)
        node_id = sb("node_id", [NB, BLOCKS], FP32)
        node_i = sb("node_i", [NB, BLOCKS], I32)
        src_16 = sb("src_16", [CHUNKS, 128], FP16)
        src_b = sb("src_b", [NB, CHUNKS * 128], FP16)
        is_src = sb("is_src", [NB, BLOCKS, 2 * 128], FP16)
        pickT = sb("pickT", [FEAT, 2 * 128], FP32)
        picked = sb("picked", [128, 2, FEAT], FP32)

        src_t = sb("src_t", [128, CHUNKS, TILES], I32)
        rel_t = sb("rel_t", [128, CHUNKS, TILES], FP32)
        ew_t = sb("ew_t", [128, CHUNKS, TILES], FP32)
        et_rows = sb("et_rows", [CHUNKS, CHUNK], BF16)
        wmin_f = sb("wmin_f", [1, CHUNKS, H], FP32)
        wmin = sb("wmin", [1, CHUNKS, H], I32)
        dmax = sb("dmax", [CHUNKS, H], FP32)
        dmin = sb("dmin", [CHUNKS, H], FP32)
        span = sb("span", [CHUNKS, H], FP32)
        wide = sb("wide", [CHUNKS, H], FP32)
        nwide = sb("nwide", [CHUNKS, 1], FP32)
        narrow = sb("narrow", [128, 1], FP32)
        general_f = sb("general_f", [1, 1], FP32)
        general = sb("general", [1, 1], I32)

        ea8_c = sb("ea8_c", [128, 2, H, K * 8], FP32)
        ea4_c = sb("ea4_c", [128, 2, H, K * COEF], FP32)
        idx_c = sb("idx_c", [128, GOT, TILES], I32)
        got = sb("got", [128, GOT, TILES, FEAT], FP32)
        xT = sb("xT", [TILES * 8, 2, 128], FP32)
        hid = sb("hid", [128, 2, TILES // 2, 128], FP32)
        onehot = sb("onehot", [128, 2, TILES, WIN], FP32)
        prod = sb("prod", [128, 2, TILES, 256], FP32)
        oc = sb("oc", [128, 2, TILES * BASES * WIN], FP32)
        sums = sb("sums", [128, BASES, 2, H, WIN], FP32)
        sel_c = sb("sel_c", [CHUNKS, GOT, 32], BF16)
        typ1 = sb("typ1", [128, 2, H * 128], FP32)
        coef = sb("coef", [128, 2, TILES, BASES], FP32)

        rows = prod[0:CHUNKS, :, :, :].rearrange("c a t f -> c (a t f)")
        src_f = rows[:, 0:1024]
        src_i = rows[:, 1024:2048].bitcast(I32)
        dst_i = rows[:, 2048:3072].bitcast(I32)
        ew_f = rows[:, 3072:4096]
        rows2 = oc[0:CHUNKS, :, :].rearrange("c a t -> c (a t)")
        dst_f = rows2[:, 0:1024]
        dst_hi = rows2[:, 1024:2048]
        et_i = rows2[:, 2048:3072].bitcast(I32)

        psum = ctx.enter_context(nc.psum_tensor("psum", [128, 8, 512], FP32))

        w_in = sem("w_in")
        lin1_in = sem("lin1_in")
        x_in = [sem(f"x_in{g}") for g in range(GROUPS)]
        src_in = sem("src_in")
        et_in = sem("et_in")
        dst_in = sem("dst_in")
        ew_in = sem("ew_in")
        zeroed = sem("zeroed")
        id0 = sem("id0")
        const = sem("const")
        acc_zero = sem("acc_zero")
        cast = sem("cast")
        consts_f = sem("consts_f")
        lin2_ready = sem("lin2_ready")
        tp_done = sem("tp_done")
        hT_copied = sem("hT_copied")
        t0_mm = sem("t0_mm")
        t0_rows = sem("t0_rows")
        d_step = sem("d_step")
        d_rows = sem("d_rows")
        tr_done = sem("tr_done")
        tr_copied = sem("tr_copied")
        cnt_done = sem("cnt_done")
        min_done = sem("min_done")
        shifted = sem("shifted")
        tables = sem("tables")
        tables1 = sem("tables1")
        ea8_in = [sem("ea8_in0"), sem("ea8_in1")]
        ea4_in = [sem("ea4_in0"), sem("ea4_in1")]

        class Norm:
            def __init__(self, n):
                self.stat = sem(f"stat{n}")
                self.aggr = sem(f"aggr{n}")
                self.var = sem(f"var{n}")
                self.root = sem(f"root{n}")
                self.inv = sem(f"inv{n}")
                self.nmr = sem(f"nmr{n}")
                self.normed = sem(f"normed{n}")
                self.stored = [sem(f"stored{n}_0"), sem(f"stored{n}_1")]

        n0, n1 = Norm(0), Norm(1)

        class Pass:
            def __init__(self, n):
                self.idx_ready = sem(f"idx_ready{n}")
                self.gathered = [sem(f"gathered{n}_{s}") for s in range(GOT)]
                self.onehot = sem(f"onehot{n}")
                self.oc_done = sem(f"oc_done{n}")
                self.agg_done = sem(f"agg_done{n}")
                self.sums_copied = sem(f"sums_copied{n}")
                self.out_done = sem(f"out_done{n}")
                self.acc_done = sem(f"acc_done{n}")

        p0, p1 = Pass(0), Pass(1)
        gather_turn = sem("gather_turn")
        turn_turn = sem("turn_turn")
        xT_done = sem("xT_done")
        xT_copied = sem("xT_copied")
        hid_done = sem("hid_done")
        silu_done = sem("silu_done")
        w_done = sem("w_done")
        prod_done = sem("prod_done")
        src16_ready = sem("src16_ready")
        src16_out = sem("src16_out")
        src_b_in = sem("src_b_in")
        hi_done = sem("hi_done")
        lo_done = sem("lo_done")
        is_src_done = sem("is_src_done")
        pick_done = sem("pick_done")
        pickT_copied = sem("pickT_copied")
        turned = sem("turned")
        picked_in = sem("picked_in")
        sel_ready = sem("sel_ready")
        typ_done = sem("typ_done")
        typ1_done = sem("typ1_done")
        cf_done = sem("cf_done")
        coef_done = sem("coef_done")
        sums_ready = sem("sums_ready")
        l0_tp = sem("l0_tp")
        l0_add = sem("l0_add")
        y_relu = sem("y_relu")
        y_tp = sem("y_tp")
        y_add = sem("y_add")
        y_out = [sem("y_out0"), sem("y_out1")]

        N_WEIGHTS = TILES + 2 + 8 + K + 2 + 1
        EARLY_POOL = 5
        AGG0 = 6
        OUT_BANK = 7
        PICK_BANK = 6

        IN_BANKS = ((0, 3), (3, 2))

        def in_bank(bank, n):
            return psum[:, bank, 0:n * 128].rearrange("p (b f) -> p b f", b=n)

        def blocks_of(t, g, n=GB):
            return t.rearrange("(b p) f -> p b f", p=NB)[:, bass.ds(g * GB, n), :]

        def chunks_done(i, r):
            return r * CHUNKS + i + 1

        def slot_uses(slot, m, r):
            return r * (PAIRS + 1 - slot) + m + 1

        def ea_loads(slot, m, r, loads):
            return 16 * (r * (PAIRS + 3 if slot == 0 else PAIRS) + m + loads)

        def quad_uses(k, q, r):
            return r * (QUADS + (k == 0)) + q + 1

        def tiles_in(k, q, r):
            return 16 * PICK_T * quad_uses(k, q, r) + (16 * r if k == 0 else 0)

        def picks(m, r):
            return r * PAIRS + m + 1

        def pairs_done(m, r):
            return r * (PAIRS + 1) + m + 1

        def pairs(eng, first, body, last):
            first(0, 0, 0)
            first(1, 1, 0)
            with eng.Fori(1, PAIRS) as m:
                for s in range(2):
                    body(m * 2 + s, s, m)
            last(LAST, 0, PAIRS)

        block = ctx.enter_context(nc.Block())

        @block.sync
        def _(sp):
            def load_x(g):
                sp.dma_start(xs[:, g * GB:(g + 1) * GB, :], blocks_of(x, g)).then_inc(x_in[g], 16)

            def load_rows(row, t, arrived):
                full = LAST * CHUNK
                sp.dma_start(row[0:LAST, :], t[0:full].rearrange("(c e) -> c e", e=CHUNK)).then_inc(arrived, 16)
                sp.dma_start(row[LAST:CHUNKS, 0:TAIL], t[full:EDGES].rearrange("(c e) -> c e", c=1)).then_inc(arrived, 16)

            load_x(0)
            load_x(1)
            sp.wait_ge(id0, 1)
            load_rows(src_i, src, src_in)
            load_x(2)
            sp.wait_ge(zeroed, 1)
            sp.dma_start(lin1[0:MUL, 0:MUL], lin1_s).then_inc(lin1_in, 16)
            for i in range(3):
                sp.dma_start(lin1[MUL + i:FEAT:3, MUL * (i + 1):MUL * (i + 2)], lin1_v).then_inc(lin1_in, 16)
            load_x(3)
            load_x(4)
            sp.wait_ge(id0, 4)
            load_rows(dst_i, dst, dst_in)
            load_rows(ew_f, eweight, ew_in)
            load_rows(et_i, etype, et_in)
            sp.wait_ge(zeroed, EARLY_POOL)
            for t in range(TILES):
                sp.dma_start(fc1_bd[8 * t:8 * t + 8, t // 2, HID * (t % 2):HID * (t % 2 + 1)], fc1).then_inc(w_in, 16)
            for n in range(2):
                sp.dma_start(fc2_bd[HID * n:HID * (n + 1), 128 * n:128 * (n + 1)], fc2).then_inc(w_in, 16)
            s0, s1 = lin2_s[0:MUL, :], lin2_s[MUL:2 * MUL, :]
            v0, v1 = lin2_v[0:MUL, :], lin2_v[MUL:2 * MUL, :]
            for n, (a, b) in enumerate(((s0, v1), (v0, s1), (v1, v1), (s1, s1))):
                sp.dma_start(lin2_a[MUL * n:MUL * (n + 1), :], a).then_inc(w_in, 16)
                sp.dma_start(lin2_b[MUL * n:MUL * (n + 1), :], b).then_inc(w_in, 16)
            for g in range(K):
                sp.dma_start(wc_bd[RELS * g:RELS * (g + 1), BASES * g:BASES * (g + 1)], w_comp).then_inc(w_in, 16)
            sp.dma_start(w_base[:, 0:4, :], weight[0:4].rearrange("b i o -> i b o")).then_inc(w_in, 16)
            sp.dma_start(w_base[:, 4:8, :], weight[4:8].rearrange("b i o -> i b o")).then_inc(w_in, 16)
            sp.dma_start(bias_c[:, :], bias.rearrange("(f a) -> f a", a=1)).then_inc(w_in, 16)

            sp.wait_ge(src16_ready, 1)
            sp.dma_start(src_row.rearrange("(c e) -> c e", e=128), src_16[:, :]).then_inc(src16_out, 16)

            for g in range(GROUPS):
                sp.wait_ge(t0_rows, 2 * (g + 1))
                sp.dma_start(blocks_of(table0, g), rows_out[:, g % 2, :, :]).then_inc(n0.stored[g % 2], 16)

            def load(i, s, m, r):
                a8 = ea8[bass.ds(i * CHUNK, CHUNK), :].rearrange("(h p k) c -> p h (k c)", h=H, k=K)
                a4 = ea4[bass.ds(i * CHUNK, CHUNK), :].rearrange("(h p k) c -> p h (k c)", h=H, k=K)
                sp.dma_start(ea8_c[:, s, :, :], a8).then_inc(ea8_in[s], 16)
                sp.dma_start(ea4_c[:, s, :, :], a4).then_inc(ea4_in[s], 16)

            def load_after(i, s, m, r):
                sp.wait_ge(xT_done, chunks_done(i - 2, r))
                sp.wait_ge(p0.oc_done, chunks_done(i - 2, r))
                load(i, s, m, r)

            def load_last(r):
                sp.wait_ge(xT_done, chunks_done(LAST - 2, r))
                sp.wait_ge(p0.oc_done, chunks_done(LAST - 2, r))
                a, b, e = LAST * CHUNK, LAST * CHUNK + HALF, EDGES - EDGES % K
                for t, c, buf, s_in in ((ea8, 8, ea8_c, ea8_in[0]), (ea4, COEF, ea4_c, ea4_in[0])):
                    sp.dma_start(buf[:, 0, 0, :], t[a:b, :].rearrange("(p k) c -> p (k c)", k=K)).then_inc(s_in, 16)
                    sp.dma_start(buf[0:TAIL1 // K, 0, 1, :], t[b:e, :].rearrange("(p k) c -> p (k c)", k=K)).then_inc(s_in, 16)
                    sp.dma_start(buf[TAIL1 // K:TAIL1 // K + 1, 0, 1, 0:(TAIL1 % K) * c],
                                 t[e:EDGES, :].rearrange("(p k) c -> p (k c)", p=1)).then_inc(s_in, 16)

            def load_pass(r):
                load(0, 0, 0, r)
                load(1, 1, 0, r)
                with sp.Fori(1, PAIRS) as m:
                    for s in range(2):
                        load_after(m * 2 + s, s, m, r)
                load_last(r)

            sp.wait_ge(src16_out, 16)
            sp.dma_start(src_b[:, :], src_row.partition_broadcast(NB)).then_inc(src_b_in, 16)

            load_pass(0)
            sp.wait_ge(tables, 1)
            many = sp.value_load(general[0:1, 0:1], min_val=0, max_val=1)
            with sp.If(many > 0):
                with sp.Fori(1, WINDOWS) as r:
                    sp.wait_ge(tables, r + 1)
                    load_pass(r)

            for g in range(GROUPS):
                sp.wait_ge(n1.normed, (g + 1) * GB)
                sp.dma_start(blocks_of(table1, g), hn[:, g % 2, :, :]).then_inc(n1.stored[g % 2], 16)
            for g in range(GROUPS):
                sp.wait_ge(y_add, 2 * (g + 1))
                sp.dma_start(blocks_of(out, g), rows_out[:, g % 2, :, :]).then_inc(y_out[g % 2], 16)
            sp.wait_ge(y_out[0], 16 * 3)
            sp.wait_ge(y_out[1], 16 * 2)

        @block.gpsimd
        def _(pool):
            for n, (row, pad) in enumerate(((src_i, 0), (dst_i, int(PAD_LOW)), (ew_f, 0.0), (et_i, 0))):
                if n:
                    pool.wait_ge(id0, n)
                nc.gpsimd.memset(row[96:CHUNKS, :], pad).then_inc(id0, 1)
            pool.wait_ge(id0, 4)
            nc.gpsimd.memset(lin1[:, :], 0.0).then_inc(zeroed, 1)
            nc.gpsimd.memset(ident[:, :], 0.0).then_inc(zeroed, 1)
            pool.wait_ge(zeroed, 2)
            nc.gpsimd.affine_select(out=ident[:, :], in_=ident[:, :], compare_op=ALU.not_equal, fill=1.0,
                                    base=0, pattern=[[-1, 128]], channel_multiplier=1).then_inc(const, 1)
            pool.wait_ge(src_in, 32)
            nc.gpsimd.tensor_copy(src_f, src_i).then_inc(cast, 1)
            nc.gpsimd.memset(fc1_bd[:, :, :], 0.0).then_inc(zeroed, 1)
            nc.gpsimd.memset(fc2_bd[:, :], 0.0).then_inc(zeroed, 1)
            nc.gpsimd.memset(wc_bd[:, :], 0.0).then_inc(zeroed, 1)
            nc.gpsimd.iota(iota_i[:, :], pattern=[[1, WIN]], base=0, channel_multiplier=0).then_inc(const, 1)
            for g in range(4):
                pool.wait_ge(const, 2 + g)
                nc.gpsimd.iota(rel_i[32 * g:32 * g + 32, :], pattern=[[1, 1]], base=0,
                               channel_multiplier=1).then_inc(const, 1)
            pool.wait_ge(const, 6)
            nc.gpsimd.memset(ones[:, :], 1.0).then_inc(const, 1)
            nc.gpsimd.memset(lin2[:, :, :], 0.0).then_inc(const, 1)
            nc.gpsimd.tensor_scalar(src_16[:, :], src_f[:, HALF + K - 1:CHUNK:K], float(-MID_NODE), None,
                                    ALU.add).then_inc(src16_ready, 1)
            nc.gpsimd.iota(node_i[:, :], pattern=[[NB, BLOCKS]], base=-MID_NODE, channel_multiplier=1).then_inc(cast, 1)
            pool.wait_ge(et_in, 32)
            nc.gpsimd.tensor_copy(et_rows[:, :], et_i).then_inc(cast, 1)
            for a in acc:
                nc.gpsimd.memset(a[:, :], 0.0).then_inc(acc_zero, 1)

            def gather_pass(p, table, r):
                def gather(i, s, m):
                    pool.wait_ge(p.idx_ready, chunks_done(i, r))
                    pool.sem_inc(gather_turn, 1)
                    for t in range(TILES):
                        pool.indirect_dma_start(
                            out=got[:, s, t, :], out_offset=None, in_=table,
                            in_offset=bass.IndirectOffsetOnAxis(ap=idx_c[:, s, t:t + 1], axis=0),
                        ).then_inc(p.gathered[s], 16)

                pairs(pool, gather, gather, gather)

            pool.wait_ge(n0.stored[0], 16 * 3)
            pool.wait_ge(n0.stored[1], 16 * 2)
            gather_pass(p0, table0, 0)
            many = pool.value_load(general[0:1, 0:1], min_val=0, max_val=1)
            with pool.If(many > 0):
                with pool.Fori(1, WINDOWS) as r:
                    gather_pass(p0, table0, r)

            pool.wait_ge(n1.stored[0], 16 * 3)
            pool.wait_ge(n1.stored[1], 16 * 2)

            def gather_pass1(r):
                def gather(i, k, tiles):
                    pool.wait_ge(p1.idx_ready, chunks_done(i, r))
                    pool.sem_inc(gather_turn, 1)
                    for t in range(tiles):
                        pool.indirect_dma_start(
                            out=got[:, k, t, :], out_offset=None, in_=table1,
                            in_offset=bass.IndirectOffsetOnAxis(ap=idx_c[:, k, t:t + 1], axis=0),
                        ).then_inc(p1.gathered[k], 16)

                with pool.Fori(0, QUADS) as q:
                    for k in range(GOT):
                        gather(q * GOT + k, k, PICK_T)
                gather(LAST, 0, TILES)

            gather_pass1(0)
            many = pool.value_load(general[0:1, 0:1], min_val=0, max_val=1)
            with pool.If(many > 0):
                with pool.Fori(1, WINDOWS) as r:
                    gather_pass1(r)

        @block.scalar
        def _(act):
            def root(n, g):
                bl = slice(g * GB, (g + 1) * GB)
                act.wait_ge(n.var, g + 1)
                nc.scalar.activation(std[:, bl], var_eps[:, bl], ACT.Sqrt).then_inc(n.root, 1)

            def normalize(n, g):
                act.wait_ge(n.nmr, g + 1)
                for j in range(GB):
                    b = g * GB + j
                    nc.scalar.activation(hn[:, g % 2, j, :], xs[:, b, :], ACT.Relu, bias=nmr[:, b:b + 1],
                                         scale=rstd[:, b:b + 1]).then_inc(n.normed, 1)

            def copy_t0(g):
                act.wait_ge(t0_mm, (g + 1) * GB)
                if g >= 2:
                    act.wait_ge(n0.stored[g % 2], 16 * (g // 2))
                for a, n in IN_BANKS:
                    nc.scalar.activation(rows_out[:, g % 2, a:a + n, :], in_bank(2 + a // 3, n)[0:NB, :, :],
                                         ACT.Copy).then_inc(t0_rows, 1)

            def copy_table(tab, n):
                for h in range(H):
                    act.wait_ge(tr_done, K * (H * n + h + 1))
                    nc.scalar.activation(
                        tab[:, :, K * h:K * (h + 1)].rearrange("p c k -> p k c"),
                        psum[:, 5 + h, 0:K * CHUNKS].rearrange("p (k c) -> p k c", k=K),
                        ACT.Copy).then_inc(tr_copied, 1)

            def take_list(p, i, s):
                nc.scalar.activation(idx_c[:, s, :], src_t[:, bass.ds(i, 1), :].rearrange("p a t -> p (a t)"),
                                     ACT.Copy).then_inc(p.idx_ready, 1)

            def copy_sums(p, n, bank, i, s, r):
                act.wait_ge(p.agg_done, chunks_done(i, r))
                nc.scalar.activation(sums[:, 0:n, s, :, :].rearrange("p n h w -> p h n w"),
                                     psum[:, bank, 0:H * n * WIN].rearrange("p (h n w) -> p h n w", h=H, n=n),
                                     ACT.Copy).then_inc(p.sums_copied, 1)

            root(n0, 0)
            normalize(n0, 0)
            root(n0, 1)
            normalize(n0, 1)
            copy_table(src_t, 0)
            act.wait_ge(tr_copied, H)
            take_list(p0, 0, 0)
            take_list(p0, 1, 1)
            for g in range(2, GROUPS):
                root(n0, g)
                act.wait_ge(tp_done, (g - 1) * GB)
                normalize(n0, g)
                copy_t0(g - 2)
            copy_t0(GROUPS - 2)
            copy_t0(GROUPS - 1)
            copy_table(rel_t, 1)
            copy_table(ew_t, 2)

            act.wait_ge(const, 8)
            act.wait_ge(w_in, 16 * N_WEIGHTS)

            def place(q, part, comp, stage, scale):
                rows_ = slice(MUL * part, MUL * (part + 1))
                dst_ = lin2[rows_, q, 0:MUL] if comp is None else lin2[rows_, q, MUL + comp:FEAT:3]
                nc.scalar.activation(dst_, stage[rows_, :], ACT.Copy, scale=scale).then_inc(lin2_ready, 1)

            place(0, 0, None, lin2_a, LIN2_SCALE)
            place(0, 2, 2, lin2_a, LIN2_SCALE)
            for i in range(3):
                place(1 + i, 1, i, lin2_a, LIN2_SCALE)
            place(3, 3, None, lin2_a, LIN2_SCALE * INV_SQRT3)
            place(4, 0, 0, lin2_b, LIN2_SCALE)
            place(4, 2, 1, lin2_b, LIN2_SCALE)
            place(5, 1, None, lin2_b, LIN2_SCALE * INV_SQRT3)
            place(6, 3, None, lin2_b, LIN2_SCALE * INV_SQRT3)

            def hidden(i, s, r):
                act.wait_ge(xT_done, chunks_done(i, r))
                nc.scalar.activation(xT[:, s, :], psum[0:TILES * 8, 0, s * 128:(s + 1) * 128],
                                     ACT.Copy).then_inc(xT_copied, 1)
                act.wait_ge(hid_done, chunks_done(i, r))
                nc.scalar.activation(hid[:, s, :, :], psum[:, 1, :].rearrange("p (v e) -> p v e", e=128),
                                     ACT.Silu, scale=FC1_SCALE).then_inc(silu_done, 1)

            def edge_pass0(r, lists=True):
                if lists:
                    take_list(p0, 0, 0)
                    take_list(p0, 1, 1)
                hidden(0, 0, r)

                def step(i, s, m, first=False):
                    hidden(i + 1, 1 - s, r)
                    if not first:
                        copy_sums(p0, Q, AGG0, i - 1, 1 - s, r)
                    act.wait_ge(p0.gathered[s], 16 * TILES * slot_uses(s, m, r))
                    act.wait_ge(prod_done, chunks_done(i, r))
                    take_list(p0, i + 2, s)

                def tail():
                    hidden(LAST, 0, r)
                    copy_sums(p0, Q, AGG0, LAST - 2, 0, r)
                    copy_sums(p0, Q, AGG0, LAST - 1, 1, r)
                    copy_sums(p0, Q, AGG0, LAST, 0, r)

                step(0, 0, 0, True)
                step(1, 1, 0)
                with act.Fori(1, PAIRS - 1) as m:
                    for s in range(2):
                        step(m * 2 + s, s, m)
                step(LAST - 2, 0, PAIRS - 1)
                tail()

            act.wait_ge(tables, 1)
            edge_pass0(0, False)
            many = act.value_load(general[0:1, 0:1], min_val=0, max_val=1)
            with act.If(many > 0):
                with act.Fori(1, WINDOWS) as r:
                    act.wait_ge(tables, r + 1)
                    edge_pass0(r)

            for g in range(GROUPS):
                root(n1, g)
                if g >= 2:
                    act.wait_ge(n1.stored[g % 2], 16 * (g // 2))
                    act.wait_ge(lo_done, g - 1)
                normalize(n1, g)
                act.wait_ge(n1.normed, (g + 1) * GB)
                nc.scalar.activation(table_16[:, g * GB:(g + 1) * GB, 0, :], hn[:, g % 2, :, :], ACT.Copy,
                                     scale=PICK_SCALE).then_inc(hi_done, 1)

            def select(i, s):
                nc.scalar.activation(sel_c[:, s, :], ident_bf[0:CHUNKS, bass.ds(i, 1)].to_broadcast([CHUNKS, 32]),
                                     ACT.Copy).then_inc(sel_ready, 1)

            def copy_pick(m, r):
                act.wait_ge(pick_done, picks(m, r) * 2)
                nc.scalar.activation(pickT[:, :], psum[:, PICK_BANK, 0:256], ACT.Copy,
                                     scale=1.0 / PICK_SCALE).then_inc(pickT_copied, 1)

            def copy_turned(m, r):
                act.wait_ge(turned, picks(m, r))
                nc.scalar.activation(picked[:, :, :], psum[:, PICK_BANK, 256:512].rearrange("p (s f) -> p s f", s=2),
                                     ACT.Copy).then_inc(picked_in, 1)

            def edge_pass1(r):
                for k in range(GOT):
                    take_list(p1, k, k)
                for k in range(GOT - 1):
                    select(k, k)
                copy_pick(0, r)

                def step(i, s, k, q, more=True, sel=True):
                    if sel:
                        act.wait_ge(typ_done, chunks_done(i, r))
                        select(i + 3, (k + 3) % GOT)
                    if more:
                        act.wait_ge(p1.gathered[k], tiles_in(k, q, r))
                        act.wait_ge(p1.agg_done, chunks_done(i, r))
                        take_list(p1, i + GOT, k)
                    copy_sums(p1, BASES, 4 + s, i, s, r)

                with act.Fori(0, QUADS - 1) as q:
                    for k in (0, 2):
                        m = q * 2 + k // 2
                        copy_turned(m, r)
                        step(q * GOT + k, 0, k, q)
                        copy_pick(m + 1, r)
                        step(q * GOT + k + 1, 1, k + 1, q)
                q = QUADS - 1
                copy_turned(PAIRS - 2, r)
                step(LAST - 4, 0, 0, q)
                copy_pick(PAIRS - 1, r)
                step(LAST - 3, 1, 1, q, more=False)
                copy_turned(PAIRS - 1, r)
                step(LAST - 2, 0, 2, q, more=False, sel=False)
                step(LAST - 1, 1, 3, q, more=False, sel=False)
                copy_sums(p1, BASES, 4, LAST, 0, r)

            edge_pass1(0)
            many = act.value_load(general[0:1, 0:1], min_val=0, max_val=1)
            with act.If(many > 0):
                with act.Fori(1, WINDOWS) as r:
                    act.wait_ge(tables1, r)
                    edge_pass1(r)

            act.wait_ge(sums_ready, 2)
            for g in range(GROUPS):
                cols = slice(g * GB * NB, (g + 1) * GB * NB)
                nc.scalar.activation(acc_y[:, cols], acc[1][:, cols], ACT.Relu, bias=bias_c[:, :]).then_inc(y_relu, 1)

        @block.vector
        def _(dve):
            def statistics(n, g):
                if g:
                    dve.wait_ge(n.aggr, g * GB)
                for j in range(GB):
                    nc.vector.bn_stats(stats[:, j, :], xs[:, g * GB + j, :]).then_inc(n.stat, 1)
                for j in range(GB):
                    dve.wait_ge(n.stat, g * GB + j + 1)
                    nc.vector.bn_aggr(mv[:, g * GB + j, :], stats[:, j, :]).then_inc(n.aggr, 1)
                bl = slice(g * GB, (g + 1) * GB)
                dve.wait_ge(n.aggr, (g + 1) * GB)
                nc.vector.tensor_scalar_add(var_eps[:, bl], mv[:, bl, 1], EPS).then_inc(n.var, 1)

            def factors(n, g):
                bl = slice(g * GB, (g + 1) * GB)
                dve.wait_ge(n.root, g + 1)
                nc.vector.reciprocal(rstd[:, bl], std[:, bl]).then_inc(n.inv, 1)
                dve.wait_ge(n.inv, g + 1)
                nc.vector.scalar_tensor_tensor(out=nmr[:, bl], in0=mv[:, bl, 0], scalar=-1.0, in1=rstd[:, bl],
                                               op0=ALU.mult, op1=ALU.mult).then_inc(n.nmr, 1)

            def copy_hT(g):
                dve.wait_ge(tp_done, (g + 1) * GB)
                if g >= 2:
                    dve.wait_ge(t0_mm, (g - 1) * GB)
                for a, n in IN_BANKS:
                    nc.vector.tensor_copy(hT[:, g % 2, a:a + n, :],
                                          in_bank(a // 3, n)[:, :, 0:NB]).then_inc(hT_copied, 1)

            for g in range(GROUPS):
                dve.wait_ge(x_in[g], 16)
                statistics(n0, g)
                if g:
                    factors(n0, g - 1)
                if g >= 2:
                    copy_hT(g - 2)
            factors(n0, GROUPS - 1)
            copy_hT(GROUPS - 2)

            dve.wait_ge(cast, 2)
            nc.vector.tensor_copy(node_id[:, :], node_i[:, :]).then_inc(consts_f, 1)
            dve.wait_ge(const, 8)
            nc.vector.tensor_copy(iota_w[:, :], iota_i[:, :]).then_inc(consts_f, 1)
            nc.vector.tensor_copy(rel_id[:, :], rel_i[:, :]).then_inc(consts_f, 1)
            nc.vector.tensor_copy(ident_bf[:, :], ident[:, :]).then_inc(consts_f, 1)

            dve.wait_ge(dst_in, 32)
            nc.vector.tensor_copy(dst_f, dst_i).then_inc(d_step, 1)
            copy_hT(GROUPS - 1)
            dve.wait_ge(d_step, 1)
            halves = dst_f.rearrange("c (h e) -> c h e", h=H)
            nc.vector.tensor_reduce(dmax[:, :], halves, AX.X, ALU.max).then_inc(d_step, 1)
            nc.vector.tensor_scalar(dst_hi, dst_f, 0.0, PAD_HIGH, ALU.is_lt, ALU.mult).then_inc(d_step, 1)
            dve.wait_ge(d_step, 3)
            nc.vector.tensor_tensor(dst_hi, dst_hi, dst_f, ALU.add).then_inc(d_step, 1)
            dve.wait_ge(d_step, 4)
            nc.vector.tensor_reduce(dmin[:, :], dst_hi.rearrange("c (h e) -> c h e", h=H), AX.X,
                                    ALU.min).then_inc(d_step, 1)
            dve.wait_ge(d_step, 5)
            nc.vector.tensor_tensor(span[:, :], dmax[:, :], dmin[:, :], ALU.subtract).then_inc(d_step, 1)
            dve.wait_ge(d_step, 6)
            nc.vector.tensor_scalar(wide[:, :], span[:, :], float(WIN), None, ALU.is_ge).then_inc(d_step, 1)
            dve.wait_ge(d_step, 7)
            nc.vector.tensor_reduce(nwide[:, :], wide[:, :], AX.X, ALU.add).then_inc(d_step, 1)
            dve.wait_ge(cnt_done, 1)
            nc.vector.tensor_scalar(narrow[:, :], psum[:, 7, 0:1], 0.5, None, ALU.is_lt).then_inc(d_step, 1)
            nc.vector.tensor_scalar(general[:, :], psum[0:1, 7, 0:1], 0.5, None, ALU.is_gt).then_inc(d_step, 1)
            dve.wait_ge(d_step, 10)
            nc.vector.tensor_scalar(dmin[:, :], dmin[:, :], narrow[0:CHUNKS, :], None, ALU.mult).then_inc(d_step, 1)
            dve.wait_ge(d_step, 11)
            for h in range(H):
                nc.vector.tensor_scalar(dst_hi[:, h * HALF:(h + 1) * HALF], dst_f[:, h * HALF:(h + 1) * HALF],
                                        dmin[:, h:h + 1], None, ALU.subtract).then_inc(d_rows, 1)

            dve.wait_ge(min_done, 2)
            for h in range(H):
                nc.vector.tensor_copy(wmin_f[:, :, h], psum[0:1, 7, 128 * (h + 1):128 * (h + 1) + CHUNKS])\
                    .then_inc(d_step, 1)
            dve.wait_ge(d_step, 13)
            nc.vector.tensor_copy(wmin[:, :, :], wmin_f[:, :, :]).then_inc(d_step, 1)
            dve.wait_ge(d_step, 14)
            dve.wait_ge(tr_copied, 6)
            dve.wait_ge(acc_zero, 2)
            nc.vector.tensor_scalar_add(narrow[0:1, :], narrow[0:1, :], 0.0).then_inc(tables, 1)

            def one_hot(p, i, s, r, free):
                if free:
                    dve.wait_ge(p.agg_done, chunks_done(i - 2, r))
                rel = rel_t[:, bass.ds(i, 1), :].rearrange("p a t -> p (a t)").unsqueeze(2)
                nc.vector.tensor_tensor(onehot[:, s, :, :], rel.broadcast_to([128, TILES, WIN]),
                                        iota_w[:, :].unsqueeze(1).broadcast_to([128, TILES, WIN]),
                                        ALU.is_equal).then_inc(p.onehot, 1)

            def spread(p, coefs, n, s, i, r):
                dve.wait_ge(p.onehot, chunks_done(i, r))
                o = oc[:, s, 0:TILES * n * WIN].rearrange("p (t n w) -> p t n w", t=TILES, n=n)
                nc.vector.tensor_tensor(o, coefs.unsqueeze(3).broadcast_to([128, TILES, n, WIN]),
                                        onehot[:, s, :, :].unsqueeze(2).broadcast_to([128, TILES, n, WIN]),
                                        ALU.mult).then_inc(p.oc_done, 1)

            def accumulate(p, a, m, r, slots=2):
                firsts = [dve.value_load(wmin[0:1, bass.ds(m * 2 + s, 1), h:h + 1].rearrange("p a b -> p (a b)"),
                                         min_val=0, max_val=NODES - 1) for s in range(slots) for h in range(H)]
                dve.wait_ge(p.out_done, pairs_done(m, r))
                for n, first in enumerate(firsts):
                    if not (isinstance(m, int) and m == 0 and n == 0 and isinstance(r, int) and r == 0):
                        dve.wait_ge(p.acc_done, (r * CHUNKS + m * 2) * H + n)
                    window = a[:, bass.ds(first, WIN)]
                    nc.vector.tensor_tensor(window, window, psum[:, OUT_BANK, n * WIN:(n + 1) * WIN],
                                            ALU.add).then_inc(p.acc_done, 1)

            def edges0(i, s, m, r, loads=1, free=True):
                one_hot(p0, i, s, r, free)
                dve.wait_ge(ea4_in[s], ea_loads(s, m, r, loads))
                spread(p0, ea4_c[:, s, :, :].rearrange("p h (k c) -> p (h k) c", c=COEF), COEF, s, i, r)
                dve.wait_ge(w_done, chunks_done(i, r))
                dve.wait_ge(p0.gathered[s], 16 * TILES * slot_uses(s, m, r))
                w = psum[:, 2 + 2 * s:4 + 2 * s, :].rearrange("p b (t f) -> p (b t) f", f=128)
                w = w.rearrange("p t (j u) -> p t j u", u=MUL)
                for n, (j, part, to) in enumerate(((0, 0, 0), (2, 3, 64), (2, 1, 128), (2, 2, 192))):
                    o = prod[:, s, :, to:to + 64].rearrange("p t (j u) -> p t j u", u=MUL)
                    v = got[:, s, :, MUL * part:MUL * (part + 1)].unsqueeze(2).broadcast_to([128, TILES, 2, MUL])
                    last = nc.vector.tensor_tensor(o, w[:, :, j:j + 2, :], v, ALU.mult)
                last.then_inc(prod_done, 1)

            def edge_pass0(r):
                edges0(0, 0, 0, r, free=False)
                edges0(1, 1, 0, r, free=False)
                edges0(2, 0, 1, r)
                edges0(3, 1, 1, r)
                accumulate(p0, acc[0], 0, r)
                with dve.Fori(2, PAIRS) as m:
                    edges0(m * 2, 0, m, r)
                    edges0(m * 2 + 1, 1, m, r)
                    accumulate(p0, acc[0], m - 1, r)
                edges0(LAST, 0, PAIRS, r, 3)
                accumulate(p0, acc[0], PAIRS - 1, r)
                accumulate(p0, acc[0], PAIRS, r, 1)
                dve.wait_ge(p0.acc_done, H * chunks_done(LAST, r))

            def shift_windows(by, done):
                nc.vector.tensor_scalar_add(rel_t[:, :, :], rel_t[:, :, :], float(-by)).then_inc(shifted, 1)
                nc.vector.tensor_scalar_add(wmin_f[:, :, :], wmin_f[:, :, :], float(by)).then_inc(shifted, 1)

            edge_pass0(0)
            many = dve.value_load(general[0:1, 0:1], min_val=0, max_val=1)
            with dve.If(many > 0):
                with dve.Fori(1, WINDOWS) as r:
                    shift_windows(WIN, None)
                    dve.wait_ge(shifted, r * 3 - 1)
                    nc.vector.tensor_copy(wmin[:, :, :], wmin_f[:, :, :]).then_inc(shifted, 1)
                    dve.wait_ge(shifted, r * 3)
                    nc.vector.tensor_scalar_add(narrow[0:1, :], narrow[0:1, :], 0.0).then_inc(tables, 1)
                    edge_pass0(r)

            dve.sem_inc(sums_ready, 1)

            def add_transposed(g, transposed, to, other, added):
                dve.wait_ge(transposed, (g + 1) * GB)
                for a, n in IN_BANKS:
                    bl = slice(g * GB + a, g * GB + a + n)
                    nc.vector.tensor_tensor(to(g, a, n), in_bank(2 * (g % 2) + a // 3, n)[0:NB, :, :], other[:, bl, :],
                                            ALU.add).then_inc(added, 1)

            def split(g):
                dve.wait_ge(hi_done, g + 1)
                bl = slice(g * GB, (g + 1) * GB)
                nc.vector.scalar_tensor_tensor(out=table_16[:, bl, 1, :], in0=hn[:, g % 2, :, :], scalar=PICK_SCALE,
                                               in1=table_16[:, bl, 0, :], op0=ALU.mult,
                                               op1=ALU.subtract).then_inc(lo_done, 1)

            for g in range(GROUPS):
                add_transposed(g, l0_tp, lambda g, a, n: xs[:, g * GB + a:g * GB + a + n, :], xs, l0_add)
                dve.wait_ge(l0_add, 2 * (g + 1))
                statistics(n1, g)
                if g:
                    factors(n1, g - 1)
                if g >= 2:
                    split(g - 2)
            factors(n1, GROUPS - 1)
            split(GROUPS - 2)
            split(GROUPS - 1)

            def type_rows(i, s, r):
                dve.wait_ge(typ_done, chunks_done(i, r))
                nc.vector.tensor_scalar(typ1[:, s, :], psum[:, 2 * s, 0:H * 128], rel_id[:, :], None,
                                        ALU.is_equal).then_inc(typ1_done, 1)

            def source_columns(m, n, r, free):
                if free:
                    dve.wait_ge(pick_done, (r * PAIRS + m) * 2 + n - 1)
                first, end = PICK_HALVES[n]
                for b in range(first, end):
                    last = nc.vector.tensor_scalar(is_src[:, b, :], src_b[:, bass.ds(m * 256, 256)],
                                                   node_id[:, b:b + 1], None, ALU.is_equal)
                last.then_inc(is_src_done, 1)

            def edges1(i, s, m, r, free=True):
                one_hot(p1, i, s, r, free)
                dve.wait_ge(cf_done, chunks_done(i, r))
                cf = psum[:, 1 + 2 * s, 0:TILES * BASES].rearrange("p (t b) -> p t b", b=BASES)
                ew = ew_t[:, bass.ds(i, 1), :].rearrange("p a t -> p (a t)").unsqueeze(2)
                nc.vector.tensor_tensor(coef[:, s, :, :], cf, ew.broadcast_to([128, TILES, BASES]),
                                        ALU.mult).then_inc(coef_done, 1)
                dve.wait_ge(coef_done, chunks_done(i, r))
                spread(p1, coef[:, s, :, :], BASES, s, i, r)

            def edge_pass1(r):
                def pair(m, pick=True):
                    edges1(m * 2, 0, m, r)
                    type_rows(m * 2 + 1, 1, r)
                    if pick:
                        source_columns(m + 1, 0, r, True)
                    edges1(m * 2 + 1, 1, m, r)
                    type_rows(m * 2 + 2, 0, r)
                    if pick:
                        source_columns(m + 1, 1, r, True)
                    accumulate(p1, acc[1], m - 1, r)

                type_rows(0, 0, r)
                type_rows(1, 1, r)
                source_columns(0, 0, r, False)
                source_columns(0, 1, r, False)
                edges1(0, 0, 0, r, False)
                edges1(1, 1, 0, r, False)
                source_columns(1, 0, r, True)
                source_columns(1, 1, r, True)
                type_rows(2, 0, r)
                pair(1)
                with dve.Fori(2, PAIRS - 1) as m:
                    pair(m)
                pair(PAIRS - 1, False)
                edges1(LAST, 0, PAIRS, r)
                accumulate(p1, acc[1], PAIRS - 1, r)
                accumulate(p1, acc[1], PAIRS, r, 1)
                dve.wait_ge(p1.acc_done, H * chunks_done(LAST, r))

            dve.wait_ge(src_b_in, 16)
            edge_pass1(0)
            many = dve.value_load(general[0:1, 0:1], min_val=0, max_val=1)
            with dve.If(many > 0):
                with dve.Fori(1, WINDOWS) as r:
                    shift_windows(-WIN, None)
                    dve.wait_ge(shifted, 3 * (WINDOWS - 1) + r * 3 - 1)
                    nc.vector.tensor_copy(wmin[:, :, :], wmin_f[:, :, :]).then_inc(shifted, 1)
                    dve.wait_ge(shifted, 3 * (WINDOWS - 1) + r * 3)
                    nc.vector.tensor_scalar_add(narrow[0:1, :], narrow[0:1, :], 0.0).then_inc(tables1, 1)
                    edge_pass1(r)

            dve.sem_inc(sums_ready, 1)

            for g in range(GROUPS):
                if g >= 2:
                    dve.wait_ge(y_out[g % 2], 16 * (g // 2))
                add_transposed(g, y_tp, lambda g, a, n: rows_out[:, g % 2, a:a + n, :], xs, y_add)

        @block.tensor
        def _(pe):
            pe.wait_ge(const, 1)

            def transpose_group(g):
                pe.wait_ge(n0.normed, (g + 1) * GB)
                if g:
                    pe.wait_ge(hT_copied, 2 * g)
                for j in range(GB):
                    nc.tensor.transpose(in_bank(j // 3, 3)[:, j % 3, 0:NB], hn[:, g % 2, j, :],
                                        ident[0:NB, 0:NB]).then_inc(tp_done, 1)

            def lin1_group(g):
                pe.wait_ge(hT_copied, 2 * (g + 1))
                if g:
                    pe.wait_ge(t0_rows, 2 * g)
                for j in range(GB):
                    nc.tensor.matmul(in_bank(2 + j // 3, 3)[0:NB, j % 3, :], hT[:, g % 2, j, :], lin1[:, :],
                                     start=True, stop=True).then_inc(t0_mm, 1)

            def count_wide():
                pe.wait_ge(d_step, 8)
                nc.tensor.matmul(psum[:, 7, 0:1], ones[0:CHUNKS, :], nwide[:, :], start=True, stop=True)\
                    .then_inc(cnt_done, 1)

            def turn_rows(row, n):
                for h in range(H):
                    if n:
                        pe.wait_ge(tr_copied, H * (n - 1) + h + 1)
                    for k in range(K):
                        nc.tensor.transpose(psum[:, 5 + h, k * CHUNKS:(k + 1) * CHUNKS],
                                            row[:, h * HALF + k:(h + 1) * HALF:K],
                                            ident[0:CHUNKS, 0:CHUNKS]).then_inc(tr_done, 1)

            transpose_group(0)
            pe.wait_ge(cast, 1)
            turn_rows(src_f, 0)
            pe.wait_ge(lin1_in, 16 * 4)
            for g in range(1, GROUPS):
                transpose_group(g)
                lin1_group(g - 1)
            lin1_group(GROUPS - 1)
            count_wide()
            pe.wait_ge(d_rows, 2)
            turn_rows(dst_hi, 1)
            pe.wait_ge(ew_in, 32)
            turn_rows(ew_f, 2)
            for h in range(H):
                nc.tensor.transpose(psum[0:1, 7, 128 * (h + 1):128 * (h + 1) + CHUNKS], dmin[:, h:h + 1],
                                    ident[0:CHUNKS, 0:CHUNKS]).then_inc(min_done, 1)

            def turn_attributes(i, s, m, r, loads=1):
                pe.wait_ge(ea8_in[s], ea_loads(s, m, r, loads))
                pe.sem_inc(turn_turn, 1)
                nc.tensor.transpose(psum[0:TILES * 8, 0, s * 128:(s + 1) * 128],
                                    ea8_c[:, s, :, :].rearrange("p h c -> p (h c)"), ident[:, :]).then_inc(xT_done, 1)

            def hidden(i, s, r):
                pe.wait_ge(xT_copied, chunks_done(i, r))
                for v in range(TILES // 2):
                    last = nc.tensor.matmul(psum[:, 1, v * 128:(v + 1) * 128], fc1_bd[:, v, :], xT[:, s, :],
                                            start=True, stop=True)
                last.then_inc(hid_done, 1)

            def edge_weights(i, s, r, free):
                pe.wait_ge(silu_done, chunks_done(i, r))
                if free:
                    pe.wait_ge(prod_done, chunks_done(i - 2, r))
                for v in range(TILES // 2):
                    last = nc.tensor.matmul(psum[:, 2 + 2 * s + v // 2, (v % 2) * 256:(v % 2 + 1) * 256],
                                            hid[:, s, v, :], fc2_bd[:, :], start=True, stop=True)
                last.then_inc(w_done, 1)

            def sums0(i, s, r, free):
                pe.wait_ge(prod_done, chunks_done(i, r))
                pe.wait_ge(p0.oc_done, chunks_done(i, r))
                if free:
                    pe.wait_ge(p0.sums_copied, chunks_done(i - 1, r))
                for h in range(H):
                    for a, q0, qn in ((0, 0, QA), (128, QA, QB)):
                        o = (h * Q + q0) * WIN
                        for k in range(K):
                            t = h * K + k
                            c = t * COEF * WIN
                            last = nc.tensor.matmul(psum[:, AGG0, o:o + qn * WIN], prod[:, s, t, a:a + 128],
                                                    oc[:, s, c:c + qn * WIN], start=(k == 0), stop=(k == K - 1))
                last.then_inc(p0.agg_done, 1)

            def outputs(p, n, w, m, r, slots=2):
                pe.wait_ge(p.sums_copied, r * CHUNKS + m * 2 + slots)
                if not (isinstance(m, int) and m == 0):
                    pe.wait_ge(p.acc_done, (r * CHUNKS + m * 2) * H)
                for q in range(n):
                    last = nc.tensor.matmul(psum[:, OUT_BANK, 0:slots * H * WIN], w[:, q, :],
                                            sums[:, q, 0:slots, :, :].rearrange("p s h w -> p (s h w)"),
                                            start=(q == 0), stop=(q == n - 1))
                last.then_inc(p.out_done, 1)

            def edge_pass0(r):
                turn_attributes(0, 0, 0, r)
                hidden(0, 0, r)
                turn_attributes(1, 1, 0, r)
                edge_weights(0, 0, r, False)
                hidden(1, 1, r)
                turn_attributes(2, 0, 1, r)
                edge_weights(1, 1, r, False)
                hidden(2, 0, r)
                sums0(0, 0, r, False)

                def even(m):
                    turn_attributes(m * 2 + 1, 1, m, r)
                    edge_weights(m * 2, 0, r, True)
                    hidden(m * 2 + 1, 1, r)
                    sums0(m * 2 - 1, 1, r, True)

                def odd(m, loads=1):
                    turn_attributes(m * 2 + 2, 0, m + 1, r, loads)
                    edge_weights(m * 2 + 1, 1, r, True)
                    outputs(p0, Q, lin2, m - 1, r)
                    hidden(m * 2 + 2, 0, r)
                    sums0(m * 2, 0, r, True)

                even(1)
                odd(1)
                with pe.Fori(2, PAIRS - 1) as m:
                    even(m)
                    odd(m)
                even(PAIRS - 1)
                odd(PAIRS - 1, 3)
                edge_weights(LAST, 0, r, True)
                sums0(LAST - 1, 1, r, True)
                outputs(p0, Q, lin2, PAIRS - 1, r)
                sums0(LAST, 0, r, True)
                outputs(p0, Q, lin2, PAIRS, r, 1)

            pe.wait_ge(w_in, 16 * N_WEIGHTS)
            pe.wait_ge(lin2_ready, 10)
            pe.wait_ge(tables, 1)
            edge_pass0(0)
            many = pe.value_load(general[0:1, 0:1], min_val=0, max_val=1)
            with pe.If(many > 0):
                with pe.Fori(1, WINDOWS) as r:
                    pe.wait_ge(tables, r + 1)
                    edge_pass0(r)

            def turn_blocks(t, g, done, added):
                if g >= 2:
                    pe.wait_ge(added, 2 * (g - 1))
                for j in range(GB):
                    b = g * GB + j
                    nc.tensor.transpose(in_bank(2 * (g % 2) + j // 3, 3)[0:NB, j % 3, :], t[:, b * NB:(b + 1) * NB],
                                        ident[:, :]).then_inc(done, 1)

            pe.wait_ge(sums_ready, 1)
            for g in range(GROUPS):
                turn_blocks(acc[0], g, l0_tp, l0_add)

            def spread_types(i, s, k4, r):
                pe.wait_ge(sel_ready, chunks_done(i, r))
                for k in range(K):
                    last = nc.tensor.matmul(psum[32 * k:32 * k + 32, 2 * s, 0:H * 128], sel_c[:, k4, :],
                                            et_rows[:, k:CHUNK:K], start=True, stop=True)
                last.then_inc(typ_done, 1)

            def coefficients(i, s, r):
                pe.wait_ge(typ1_done, chunks_done(i, r))
                for h in range(H):
                    last = nc.tensor.matmul(psum[:, 1 + 2 * s, 32 * h:32 * (h + 1)],
                                            typ1[:, s, 128 * h:128 * (h + 1)], wc_bd[:, :], start=True, stop=True)
                last.then_inc(cf_done, 1)

            def sums1(i, s, m, k4, q, r, free, last_chunk=False):
                if last_chunk:
                    pe.wait_ge(p1.gathered[0], tiles_in(0, QUADS, r) + 16)
                else:
                    pe.wait_ge(p1.gathered[k4], tiles_in(k4, q, r))
                    pe.wait_ge(picked_in, picks(m, r))
                pe.wait_ge(p1.oc_done, chunks_done(i, r))
                if free:
                    pe.wait_ge(p1.sums_copied, chunks_done(i - 2, r))
                n = BASES * WIN
                for h in range(H):
                    for k in range(K):
                        t = h * K + k
                        rows_ = got[:, k4, t, :] if t != PICK_T or last_chunk else picked[:, s, :]
                        last = nc.tensor.matmul(psum[:, 4 + s, h * n:(h + 1) * n], rows_,
                                                oc[:, s, t * n:(t + 1) * n], start=(k == 0), stop=(k == K - 1))
                last.then_inc(p1.agg_done, 1)

            def pick(m, n, r, free):
                if free and n == 0:
                    pe.wait_ge(picked_in, picks(m - 1, r))
                pe.wait_ge(is_src_done, (r * PAIRS + m) * 2 + n + 1)
                first, end = PICK_HALVES[n]
                for b in range(first, end):
                    for part in range(2):
                        last = nc.tensor.matmul(psum[:, PICK_BANK, 0:256], table_16[:, b, part, :], is_src[:, b, :],
                                                start=(b == 0 and part == 0), stop=(b == BLOCKS - 1 and part == 1))
                last.then_inc(pick_done, 1)

            def turn_picked(m, r):
                pe.wait_ge(pickT_copied, picks(m, r))
                for s in range(2):
                    last = nc.tensor.transpose(psum[:, PICK_BANK, 256 + 128 * s:256 + 128 * (s + 1)],
                                               pickT[:, 128 * s:128 * (s + 1)], ident[:, :])
                last.then_inc(turned, 1)

            def edge_pass1(r):
                spread_types(0, 0, 0, r)
                spread_types(1, 1, 1, r)
                coefficients(0, 0, r)
                pick(0, 0, r, False)
                pick(0, 1, r, False)
                turn_picked(0, r)
                spread_types(2, 0, 2, r)
                coefficients(1, 1, r)
                pick(1, 0, r, True)
                sums1(0, 0, 0, 0, 0, r, False)
                pick(1, 1, r, True)

                def even(m, k, q, free=True):
                    spread_types(m * 2 + 1, 1, k + 1, r)
                    coefficients(m * 2, 0, r)
                    sums1(m * 2 - 1, 1, m - 1, (k - 1) % GOT, q - (k == 0), r, free)
                    turn_picked(m, r)

                def odd(m, k, q, more=True):
                    spread_types(m * 2 + 2, 0, (k + 2) % GOT, r)
                    coefficients(m * 2 + 1, 1, r)
                    outputs(p1, BASES, w_base, m - 1, r)
                    if more:
                        pick(m + 1, 0, r, True)
                    sums1(m * 2, 0, m, k, q, r, True)
                    if more:
                        pick(m + 1, 1, r, True)

                even(1, 2, 0, False)
                odd(1, 2, 0)
                with pe.Fori(1, QUADS - 1) as q:
                    for k in (0, 2):
                        even(q * 2 + k // 2, k, q)
                        odd(q * 2 + k // 2, k, q)
                q = QUADS - 1
                even(PAIRS - 2, 0, q)
                odd(PAIRS - 2, 0, q)
                even(PAIRS - 1, 2, q)
                odd(PAIRS - 1, 2, q, False)
                coefficients(LAST, 0, r)
                sums1(LAST - 1, 1, PAIRS - 1, 3, q, r, True)
                outputs(p1, BASES, w_base, PAIRS - 1, r)
                sums1(LAST, 0, PAIRS, 0, QUADS, r, True, True)
                outputs(p1, BASES, w_base, PAIRS, r, 1)

            edge_pass1(0)
            many = pe.value_load(general[0:1, 0:1], min_val=0, max_val=1)
            with pe.If(many > 0):
                with pe.Fori(1, WINDOWS) as r:
                    pe.wait_ge(tables1, r)
                    edge_pass1(r)

            for g in range(GROUPS):
                pe.wait_ge(y_relu, g + 1)
                turn_blocks(acc_y, g, y_tp, y_add)


_INS = ["x", "src", "dst", "edge_attr_4", "edge_attr_8", "edge_type_32", "edge_weight1", "L0_gnn_w_lin1_s",
        "L0_gnn_w_lin1_v", "L0_gnn_fc_w1", "L0_gnn_fc_w2", "L0_gnn_w_lin2_s", "L0_gnn_w_lin2_v",
        "L1_gnn_weight", "L1_gnn_w_comp", "L1_gnn_bias_param"]


def kernel(**inputs):
    import numpy as _np
    import concourse.bacc as _bacc
    from concourse.bass_utils import run_bass_kernel_spmd as _run

    nc = _bacc.Bacc("TRN2", target_bir_lowering=False, num_devices=1)
    arrays, args = {}, []
    for name in _INS:
        a = _np.ascontiguousarray(inputs[name])
        if name == "edge_weight1":
            a = a.reshape(-1)
        arrays[f"in_{name}"] = a
        args.append(nc.dram_tensor(f"in_{name}", a.shape, mybir.dt.from_np(a.dtype), kind="ExternalInput").ap())
    for name in ("table0", "table1"):
        args.append(nc.dram_tensor(name, [NODES, FEAT], FP32, kind="Internal").ap())
    args.append(nc.dram_tensor("src_row", [CHUNKS * 128], FP16, kind="Internal").ap())
    args.append(nc.dram_tensor("out_0", [NODES, FEAT], FP32, kind="ExternalOutput").ap())
    gnn_two_layers(nc, *args)
    r = _run(nc, [arrays], core_ids=[0])
    return r.results[0]["out_0"]
```

```python
import concourse.bass as bass
from concourse import mybir
from contextlib import ExitStack

FP32 = mybir.dt.float32
BF16 = mybir.dt.bfloat16
FP16 = mybir.dt.float16
I32 = mybir.dt.int32
ALU = mybir.AluOpType
ACT = mybir.ActivationFunctionType
AX = mybir.AxisListType

NODES = 3125
FEAT = 128
EDGES = 103125
MUL = 32
HID = 64
BASES = 8
RELS = 32

NB = 125
BLOCKS = NODES // NB
GB = 5
GROUPS = BLOCKS // GB

SPRAYED = ((0, 112), (112, NB))
MOVED = 16 * len(SPRAYED)

WIN = 24
HALF = 512
K = HALF // 128
H = 2
TILES = H * K
CHUNK = H * HALF
CHUNKS = -(-EDGES // CHUNK)
TAIL = EDGES - (CHUNKS - 1) * CHUNK
TAIL1 = TAIL - HALF
LAST = CHUNKS - 1
PAIRS = CHUNKS // 2
assert HALF < TAIL < CHUNK and CHUNKS % 2 == 1 and CHUNKS <= 128
WINDOWS = -(-NODES // WIN)
ACC_N = NODES + WIN - 1

COEF = 4
SUMS0 = 3 + COEF

PICK_T = TILES - 1
PICK_SCALE = 4096.0
MID_NODE = NODES // 2
PICK_HALVES = ((0, 13), (13, BLOCKS))
UNPICKED = 2
PICKED0 = PAIRS - 1 - 2 * UNPICKED
assert PICK_SCALE * FEAT ** 0.5 < 65504 and MID_NODE < 2048
GOT = 4
QUADS = CHUNKS // GOT

EPS = 1e-5
SILU_NORM = 1.6791767923989418
NUM_NEIGHBORS = 16.0
FC1_SCALE = 8 ** -0.5
LIN2_SCALE = MUL ** -0.5 * SILU_NORM * HID ** -0.5 * NUM_NEIGHBORS ** -0.5 * (2 * MUL) ** -0.5
INV_SQRT3 = 3.0 ** -0.5
PAD_LOW = -1.0
PAD_HIGH = 8192.0


def gnn_two_layers(nc, x, src, dst, ea4, ea8, etype, eweight, lin1_s, lin1_v, fc1, fc2, lin2_s, lin2_v,
                   weight, w_comp, bias, table0, table1, src_row, out):
    ctx = ExitStack()
    with ctx:
        def sb(name, shape, dt):
            return ctx.enter_context(nc.sbuf_tensor(name, shape, dt))

        def sem(name):
            return ctx.enter_context(nc.semaphore(name))

        ident = sb("ident", [128, 128], FP32)
        ident_bf = sb("ident_bf", [128, 128], BF16)
        iota_i = sb("iota_i", [128, WIN], I32)
        iota_w = sb("iota_w", [128, WIN], FP32)
        rel_i = sb("rel_i", [128, 1], I32)
        rel_id = sb("rel_id", [128, 1], FP32)
        ones = sb("ones", [128, 128], FP32)

        lin1 = sb("lin1", [FEAT, FEAT], FP32)
        fc1_bd = sb("fc1_bd", [TILES * 8, TILES // 2, 128], FP32)
        fc2_bd = sb("fc2_bd", [128, 256], FP32)
        lin2_a = sb("lin2_a", [128, MUL], FP32)
        lin2_b = sb("lin2_b", [128, MUL], FP32)
        lin2 = sb("lin2", [128, COEF, FEAT], FP32)
        wc_bd = sb("wc_bd", [128, K * BASES], FP32)
        w_base = sb("w_base", [FEAT, BASES, FEAT], FP32)
        bias_c = sb("bias_c", [FEAT, 1], FP32)

        xs = sb("xs", [NB, BLOCKS, FEAT], FP32)
        stats = sb("stats", [NB, GB, 6], FP32)
        mv = sb("mv", [NB, BLOCKS, 2], FP32)
        var_eps = sb("var_eps", [NB, BLOCKS], FP32)
        std = sb("std", [NB, BLOCKS], FP32)
        rstd = sb("rstd", [NB, BLOCKS], FP32)
        nmr = sb("nmr", [NB, BLOCKS], FP32)
        hn = sb("hn", [NB, GROUPS, GB, FEAT], FP32)
        hT = sb("hT", [FEAT, 2, GB, NB], FP32)
        rows_out = sb("rows_out", [NB, 2, GB, FEAT], FP32)
        acc = [sb(f"acc{n}", [FEAT, ACC_N], FP32) for n in range(2)]

        table_16 = sb("table_16", [NB, BLOCKS, 2, FEAT], FP16)
        node_id = sb("node_id", [NB, BLOCKS], FP32)
        node_i = sb("node_i", [NB, BLOCKS], I32)
        src_16 = sb("src_16", [CHUNKS, 128], FP16)
        src_b = sb("src_b", [128, CHUNKS * 128], FP16)
        is_src = sb("is_src", [NB, BLOCKS, 2 * 128], FP16)
        pickT = sb("pickT", [FEAT, 2 * 128], FP32)
        picked = sb("picked", [128, 2, FEAT], FP32)

        src_t = sb("src_t", [128, CHUNKS, TILES], I32)
        rel_t = sb("rel_t", [128, CHUNKS, TILES], FP32)
        ew_t = sb("ew_t", [128, CHUNKS, TILES], FP32)
        et_rows = sb("et_rows", [CHUNKS, CHUNK], BF16)
        wmin_f = sb("wmin_f", [1, CHUNKS, H], FP32)
        wmin = sb("wmin", [1, CHUNKS, H], I32)
        dmax = sb("dmax", [CHUNKS, H], FP32)
        dmin = sb("dmin", [CHUNKS, H], FP32)
        span = sb("span", [CHUNKS, H], FP32)
        wide = sb("wide", [CHUNKS, H], FP32)
        nwide = sb("nwide", [CHUNKS, 1], FP32)
        narrow = sb("narrow", [128, 1], FP32)
        general_f = sb("general_f", [1, 1], FP32)
        general = sb("general", [1, 1], I32)

        ea8_c = sb("ea8_c", [128, 2, H, K * 8], FP32)
        ea4_c = sb("ea4_c", [128, 2, H, K * COEF], FP32)
        idx_c = sb("idx_c", [128, GOT, TILES], I32)
        got = sb("got", [128, GOT, TILES, FEAT], FP32)
        xT = sb("xT", [TILES * 8, 2, 128], FP32)
        hid = sb("hid", [128, 2, TILES // 2, 128], FP32)
        onehot = sb("onehot", [128, 2, TILES, WIN], FP32)
        prod = sb("prod", [128, 2, TILES, 256], FP32)
        oc = sb("oc", [128, 2, TILES * BASES * WIN], FP32)
        sums = sb("sums", [128, BASES * 2 * H * WIN], FP32)
        sel_c = sb("sel_c", [CHUNKS, GOT, 32], BF16)
        typ1 = sb("typ1", [128, 2, H * 128], FP32)
        coef = sb("coef", [128, 2, TILES, BASES], FP32)

        acc_y = got.rearrange("p a t f -> p (a t f)")[:, 0:NODES]

        rows = prod[0:CHUNKS, :, :, :].rearrange("c a t f -> c (a t f)")
        src_f = rows[:, 0:1024]
        src_i = rows[:, 1024:2048].bitcast(I32)
        dst_i = rows[:, 2048:3072].bitcast(I32)
        ew_f = rows[:, 3072:4096]
        rows2 = oc[0:CHUNKS, :, :].rearrange("c a t -> c (a t)")
        dst_f = rows2[:, 0:1024]
        dst_hi = rows2[:, 1024:2048]
        et_i = rows2[:, 2048:3072].bitcast(I32)

        psum = ctx.enter_context(nc.psum_tensor("psum", [128, 8, 512], FP32))

        w_in = sem("w_in")
        w1_in = sem("w1_in")
        lin1_in = sem("lin1_in")
        x_in = [sem(f"x_in{g}") for g in range(GROUPS)]
        src_in = sem("src_in")
        et_in = sem("et_in")
        dst_in = sem("dst_in")
        ew_in = sem("ew_in")
        zeroed = sem("zeroed")
        id0 = sem("id0")
        const = sem("const")
        acc_zero = sem("acc_zero")
        cast = sem("cast")
        consts_f = sem("consts_f")
        lin2_ready = sem("lin2_ready")
        tp_done = sem("tp_done")
        hT_copied = sem("hT_copied")
        t0_mm = sem("t0_mm")
        t0_rows = sem("t0_rows")
        d_step = sem("d_step")
        d_rows = sem("d_rows")
        tr_done = sem("tr_done")
        tr_copied = sem("tr_copied")
        cnt_done = sem("cnt_done")
        min_done = sem("min_done")
        shifted = sem("shifted")
        tables = sem("tables")
        tables1 = sem("tables1")
        ea8_in = [sem("ea8_in0"), sem("ea8_in1")]
        ea4_in = [sem("ea4_in0"), sem("ea4_in1")]

        class Norm:
            def __init__(self, n):
                self.stat = sem(f"stat{n}")
                self.aggr = sem(f"aggr{n}")
                self.var = sem(f"var{n}")
                self.root = sem(f"root{n}")
                self.inv = sem(f"inv{n}")
                self.nmr = sem(f"nmr{n}")
                self.hi_done = sem(f"hi_done{n}")
                self.lo_done = sem(f"lo_done{n}")
                self.normed = sem(f"normed{n}")
                self.stored = [sem(f"stored{n}_0"), sem(f"stored{n}_1")]

        n0, n1 = Norm(0), Norm(1)

        class Pass:
            def __init__(self, layer, n, per):
                self.per = per
                self.sums = sums[:, :].rearrange("p (n s h w) -> p n s h w", n=n, s=per, h=H)
                n = layer
                self.idx_ready = sem(f"idx_ready{n}")
                self.gathered = [sem(f"gathered{n}_{s}") for s in range(GOT)]
                self.onehot = sem(f"onehot{n}")
                self.oc_done = sem(f"oc_done{n}")
                self.agg_done = sem(f"agg_done{n}")
                self.sums_copied = sem(f"sums_copied{n}")
                self.out_done = sem(f"out_done{n}")
                self.acc_done = sem(f"acc_done{n}")
                self.is_src_done = sem(f"is_src_done{n}")
                self.pick_done = sem(f"pick_done{n}")
                self.pickT_copied = sem(f"pickT_copied{n}")
                self.picked_in = sem(f"picked_in{n}")

        p0, p1 = Pass(0, COEF, GOT), Pass(1, BASES, 2)
        assert COEF * GOT == BASES * 2
        gather_turn = sem("gather_turn")
        turn_turn = sem("turn_turn")
        xT_done = sem("xT_done")
        xT_copied = sem("xT_copied")
        hid_done = sem("hid_done")
        silu_done = sem("silu_done")
        w_done = sem("w_done")
        prod_done = sem("prod_done")
        src16_ready = sem("src16_ready")
        src16_out = sem("src16_out")
        src_b_in = sem("src_b_in")
        turned = sem("turned")
        sel_ready = sem("sel_ready")
        typ_done = sem("typ_done")
        typ1_done = sem("typ1_done")
        cf_done = sem("cf_done")
        coef_done = sem("coef_done")
        sums_ready = sem("sums_ready")
        l0_tp = sem("l0_tp")
        l0_add = sem("l0_add")
        y_relu = sem("y_relu")
        y_tp = sem("y_tp")
        y_add = sem("y_add")
        y_out = sem("y_out")

        N_WEIGHTS = TILES + 2 + 8
        EARLY_POOL = 5
        AGG0 = 6
        OUT_BANK = 7
        PICK_BANK = 6
        PICK_AT = 256
        ROWS_AT = H * SUMS0 * WIN
        assert ROWS_AT + FEAT <= 512

        IN_BANKS = ((0, 3), (3, 2))

        def in_bank(bank, n):
            return psum[:, bank, 0:n * 128].rearrange("p (b f) -> p b f", b=n)

        def blocks_of(t, g, p0_, p1_):
            return t.rearrange("(b p) f -> p b f", p=NB)[p0_:p1_, g * GB:(g + 1) * GB, :]

        def chunks_done(i, r):
            return r * CHUNKS + i + 1

        def ea_loads(slot, m, r, loads):
            return 16 * (r * (PAIRS + 3 if slot == 0 else PAIRS) + m + loads)

        def quad_uses(k, q, r):
            return r * (QUADS + (k == 0)) + q + 1

        def tiles_in0(k, q, r):
            if k % 2 == 0:
                return 16 * TILES * quad_uses(k, q, r)
            first = k == 1
            last = max(q + 1 - (QUADS - UNPICKED), 0) if isinstance(q, int) else 0
            return 16 * (r * (PICK_T * QUADS + first + UNPICKED) + PICK_T * (q + 1) + first + last)

        def tiles_in(k, q, r):
            return 16 * PICK_T * quad_uses(k, q, r) + (16 * r if k == 0 else 0)

        def picks_before(p, m, r):
            return r * PAIRS + m if p is p1 else r * PICKED0 + m - 1

        def picks(p, m, r):
            return picks_before(p, m, r) + 1

        def outs_done(p, u, r):
            return r * (CHUNKS // p.per + 1) + u + 1

        block = ctx.enter_context(nc.Block())

        @block.sync
        def _(sp):
            def load_x(g):
                for a, b in SPRAYED:
                    sp.dma_start(xs[a:b, g * GB:(g + 1) * GB, :], blocks_of(x, g, a, b)).then_inc(x_in[g], 16)

            def load_rows(row, t, arrived):
                full = LAST * CHUNK
                sp.dma_start(row[0:LAST, :], t[0:full].rearrange("(c e) -> c e", e=CHUNK)).then_inc(arrived, 16)
                sp.dma_start(row[LAST:CHUNKS, 0:TAIL], t[full:EDGES].rearrange("(c e) -> c e", c=1)).then_inc(arrived, 16)

            def store_table0(g):
                sp.wait_ge(t0_rows, 2 * (g + 1))
                for a, b in SPRAYED:
                    sp.dma_start(blocks_of(table0, g, a, b), rows_out[a:b, g % 2, :, :]).then_inc(n0.stored[g % 2], 16)

            load_x(0)
            load_x(1)
            sp.wait_ge(id0, 1)
            load_rows(src_i, src, src_in)
            load_x(2)
            sp.wait_ge(zeroed, 1)
            sp.dma_start(lin1[0:MUL, 0:MUL], lin1_s).then_inc(lin1_in, 16)
            for i in range(3):
                sp.dma_start(lin1[MUL + i:FEAT:3, MUL * (i + 1):MUL * (i + 2)], lin1_v).then_inc(lin1_in, 16)
            load_x(3)
            load_x(4)
            sp.wait_ge(id0, 4)
            load_rows(dst_i, dst, dst_in)
            load_rows(ew_f, eweight, ew_in)
            load_rows(et_i, etype, et_in)
            sp.wait_ge(zeroed, EARLY_POOL)
            for t in range(TILES):
                sp.dma_start(fc1_bd[8 * t:8 * t + 8, t // 2, HID * (t % 2):HID * (t % 2 + 1)], fc1).then_inc(w_in, 16)
            store_table0(0)
            for n in range(2):
                sp.dma_start(fc2_bd[HID * n:HID * (n + 1), 128 * n:128 * (n + 1)], fc2).then_inc(w_in, 16)
            s0, s1 = lin2_s[0:MUL, :], lin2_s[MUL:2 * MUL, :]
            v0, v1 = lin2_v[0:MUL, :], lin2_v[MUL:2 * MUL, :]
            for n, (a, b) in enumerate(((s0, v0), (v1, s1), (v1, s1), (v1, s1))):
                sp.dma_start(lin2_a[MUL * n:MUL * (n + 1), :], a).then_inc(w_in, 16)
                sp.dma_start(lin2_b[MUL * n:MUL * (n + 1), :], b).then_inc(w_in, 16)
                if n == 1:
                    store_table0(1)
            sp.wait_ge(src16_ready, 1)
            sp.dma_start(src_row.rearrange("(c e) -> c e", e=128), src_16[:, :]).then_inc(src16_out, 16)
            for g in range(2, GROUPS):
                store_table0(g)
            def load(i, s, r, free=True):
                a8 = ea8[bass.ds(i * CHUNK, CHUNK), :].rearrange("(h p k) c -> p h (k c)", h=H, k=K)
                a4 = ea4[bass.ds(i * CHUNK, CHUNK), :].rearrange("(h p k) c -> p h (k c)", h=H, k=K)
                if free:
                    sp.wait_ge(xT_done, chunks_done(i - 2, r))
                sp.dma_start(ea8_c[:, s, :, :], a8).then_inc(ea8_in[s], 16)
                if free:
                    sp.wait_ge(p0.oc_done, chunks_done(i - 2, r))
                sp.dma_start(ea4_c[:, s, :, :], a4).then_inc(ea4_in[s], 16)

            def load_last(r):
                sp.wait_ge(xT_done, chunks_done(LAST - 2, r))
                sp.wait_ge(p0.oc_done, chunks_done(LAST - 2, r))
                a, b, e = LAST * CHUNK, LAST * CHUNK + HALF, EDGES - EDGES % K
                for t, c, buf, s_in in ((ea8, 8, ea8_c, ea8_in[0]), (ea4, COEF, ea4_c, ea4_in[0])):
                    sp.dma_start(buf[:, 0, 0, :], t[a:b, :].rearrange("(p k) c -> p (k c)", k=K)).then_inc(s_in, 16)
                    sp.dma_start(buf[0:TAIL1 // K, 0, 1, :], t[b:e, :].rearrange("(p k) c -> p (k c)", k=K)).then_inc(s_in, 16)
                    sp.dma_start(buf[TAIL1 // K:TAIL1 // K + 1, 0, 1, 0:(TAIL1 % K) * c],
                                 t[e:EDGES, :].rearrange("(p k) c -> p (k c)", p=1)).then_inc(s_in, 16)

            def load_weights1():
                for g in range(K):
                    sp.dma_start(wc_bd[RELS * g:RELS * (g + 1), BASES * g:BASES * (g + 1)], w_comp)\
                        .then_inc(w1_in, 16)
                sp.dma_start(w_base[:, 0:4, :], weight[0:4].rearrange("b i o -> i b o")).then_inc(w1_in, 16)
                sp.dma_start(w_base[:, 4:8, :], weight[4:8].rearrange("b i o -> i b o")).then_inc(w1_in, 16)
                sp.dma_start(bias_c[:, :], bias.rearrange("(f a) -> f a", a=1)).then_inc(w1_in, 16)

            def load_pass(r):
                load(0, 0, r, False)
                load(1, 1, r, False)
                if isinstance(r, int):
                    sp.wait_ge(src16_out, 16)
                    sp.dma_start(src_b[:, :], src_row.partition_broadcast(128)).then_inc(src_b_in, 16)
                    load_weights1()
                with sp.Fori(1, PAIRS) as m:
                    for s in range(2):
                        load(m * 2 + s, s, r)
                load_last(r)

            load_pass(0)
            sp.wait_ge(tables, 1)
            many = sp.value_load(general[0:1, 0:1], min_val=0, max_val=1)
            with sp.If(many > 0):
                with sp.Fori(1, WINDOWS) as r:
                    sp.wait_ge(tables, r + 1)
                    load_pass(r)

            for g in range(GROUPS):
                sp.wait_ge(n1.normed, (g + 1) * GB)
                for a, b in SPRAYED:
                    sp.dma_start(blocks_of(table1, g, a, b), hn[a:b, g, :, :]).then_inc(n1.stored[g % 2], 16)
            for g in range(GROUPS):
                sp.wait_ge(y_add, 2 * (g + 1))
                for a, b in SPRAYED:
                    sp.dma_start(blocks_of(out, g, a, b), hn[a:b, g, :, :]).then_inc(y_out, 16)
            sp.wait_ge(y_out, MOVED * GROUPS)

        @block.gpsimd
        def _(pool):
            for n, (row, pad) in enumerate(((src_i, 0), (dst_i, int(PAD_LOW)), (ew_f, 0.0), (et_i, 0))):
                if n:
                    pool.wait_ge(id0, n)
                nc.gpsimd.memset(row[96:CHUNKS, :], pad).then_inc(id0, 1)
            pool.wait_ge(id0, 4)
            nc.gpsimd.memset(lin1[:, :], 0.0).then_inc(zeroed, 1)
            nc.gpsimd.memset(ident[:, :], 0.0).then_inc(zeroed, 1)
            pool.wait_ge(zeroed, 2)
            nc.gpsimd.affine_select(out=ident[:, :], in_=ident[:, :], compare_op=ALU.not_equal, fill=1.0,
                                    base=0, pattern=[[-1, 128]], channel_multiplier=1).then_inc(const, 1)
            pool.wait_ge(src_in, 32)
            nc.gpsimd.tensor_copy(src_f, src_i).then_inc(cast, 1)
            nc.gpsimd.memset(fc1_bd[:, :, :], 0.0).then_inc(zeroed, 1)
            nc.gpsimd.memset(fc2_bd[:, :], 0.0).then_inc(zeroed, 1)
            nc.gpsimd.memset(wc_bd[:, :], 0.0).then_inc(zeroed, 1)
            nc.gpsimd.iota(iota_i[:, :], pattern=[[1, WIN]], base=0, channel_multiplier=0).then_inc(const, 1)
            for g in range(4):
                pool.wait_ge(const, 2 + g)
                nc.gpsimd.iota(rel_i[32 * g:32 * g + 32, :], pattern=[[1, 1]], base=0,
                               channel_multiplier=1).then_inc(const, 1)
            pool.wait_ge(const, 6)
            nc.gpsimd.memset(ones[:, :], 1.0).then_inc(const, 1)
            nc.gpsimd.memset(lin2[:, :, :], 0.0).then_inc(const, 1)
            nc.gpsimd.tensor_scalar(src_16[:, :], src_f[:, HALF + K - 1:CHUNK:K], float(-MID_NODE), None,
                                    ALU.add).then_inc(src16_ready, 1)
            nc.gpsimd.iota(node_i[:, :], pattern=[[NB, BLOCKS]], base=-MID_NODE, channel_multiplier=1).then_inc(cast, 1)
            pool.wait_ge(et_in, 32)
            nc.gpsimd.tensor_copy(et_rows[:, :], et_i).then_inc(cast, 1)
            for a in acc:
                nc.gpsimd.memset(a[:, :], 0.0).then_inc(acc_zero, 1)

            def gather(p, table, i, k, tiles, r):
                pool.wait_ge(p.idx_ready, chunks_done(i, r))
                pool.sem_inc(gather_turn, 1)
                for t in range(tiles):
                    pool.indirect_dma_start(
                        out=got[:, k, t, :], out_offset=None, in_=table,
                        in_offset=bass.IndirectOffsetOnAxis(ap=idx_c[:, k, t:t + 1], axis=0),
                    ).then_inc(p.gathered[k], 16)

            def gather_pass0(r):
                gather(p0, table0, 0, 0, TILES, r)
                gather(p0, table0, 1, 1, TILES, r)
                gather(p0, table0, 2, 2, TILES, r)
                gather(p0, table0, 3, 3, PICK_T, r)
                with pool.Fori(1, QUADS - UNPICKED) as q:
                    for k in range(GOT):
                        gather(p0, table0, q * GOT + k, k, PICK_T if k % 2 else TILES, r)
                with pool.Fori(QUADS - UNPICKED, QUADS) as q:
                    for k in range(GOT):
                        gather(p0, table0, q * GOT + k, k, TILES, r)
                gather(p0, table0, LAST, 0, TILES, r)

            pool.wait_ge(n0.stored[0], MOVED * 3)
            pool.wait_ge(n0.stored[1], MOVED * 2)
            gather_pass0(0)
            many = pool.value_load(general[0:1, 0:1], min_val=0, max_val=1)
            with pool.If(many > 0):
                with pool.Fori(1, WINDOWS) as r:
                    gather_pass0(r)

            pool.wait_ge(n1.stored[0], MOVED * 3)
            pool.wait_ge(n1.stored[1], MOVED * 2)

            def gather_pass1(r):
                with pool.Fori(0, QUADS) as q:
                    for k in range(GOT):
                        gather(p1, table1, q * GOT + k, k, PICK_T, r)
                gather(p1, table1, LAST, 0, TILES, r)

            gather_pass1(0)
            many = pool.value_load(general[0:1, 0:1], min_val=0, max_val=1)
            with pool.If(many > 0):
                with pool.Fori(1, WINDOWS) as r:
                    gather_pass1(r)

        @block.scalar
        def _(act):
            def root(n, g):
                bl = slice(g * GB, (g + 1) * GB)
                act.wait_ge(n.var, g + 1)
                nc.scalar.activation(std[:, bl], var_eps[:, bl], ACT.Sqrt).then_inc(n.root, 1)

            def normalize(n, g):
                act.wait_ge(n.nmr, g + 1)
                for j in range(GB):
                    b = g * GB + j
                    nc.scalar.activation(hn[:, g, j, :], xs[:, b, :], ACT.Relu, bias=nmr[:, b:b + 1],
                                         scale=rstd[:, b:b + 1]).then_inc(n.normed, 1)

            def leading_part(n, g):
                act.wait_ge(n.normed, (g + 1) * GB)
                nc.scalar.activation(table_16[:, g * GB:(g + 1) * GB, 0, :], hn[:, g, :, :], ACT.Copy,
                                     scale=PICK_SCALE).then_inc(n.hi_done, 1)

            def copy_pick(p, n, bank, at, m, r):
                act.wait_ge(p.pick_done, picks(p, m, r) * len(PICK_HALVES))
                nc.scalar.activation(pickT[:, 0:n], psum[:, bank, at:at + n], ACT.Copy,
                                     scale=1.0 / PICK_SCALE).then_inc(p.pickT_copied, 1)

            def copy_t0(g):
                act.wait_ge(t0_mm, (g + 1) * GB)
                if g >= 2:
                    act.wait_ge(n0.stored[g % 2], MOVED * (g // 2))
                for a, n in IN_BANKS:
                    nc.scalar.activation(rows_out[:, g % 2, a:a + n, :], in_bank(2 + a // 3, n)[0:NB, :, :],
                                         ACT.Copy).then_inc(t0_rows, 1)

            def copy_table(tab, n):
                for h in range(H):
                    act.wait_ge(tr_done, K * (H * n + h + 1))
                    nc.scalar.activation(
                        tab[:, :, K * h:K * (h + 1)].rearrange("p c k -> p k c"),
                        psum[:, 5 + h, 0:K * CHUNKS].rearrange("p (k c) -> p k c", k=K),
                        ACT.Copy).then_inc(tr_copied, 1)

            def take_list(p, i, s):
                nc.scalar.activation(idx_c[:, s, :], src_t[:, bass.ds(i, 1), :].rearrange("p a t -> p (a t)"),
                                     ACT.Copy).then_inc(p.idx_ready, 1)

            def copy_sums(p, n, of, bank, i, s, r):
                act.wait_ge(p.agg_done, chunks_done(i, r))
                nc.scalar.activation(p.sums[:, :, s, :, :].rearrange("p n h w -> p h n w"),
                                     psum[:, bank, 0:H * of * WIN]
                                     .rearrange("p (h n w) -> p h n w", h=H, n=of)[:, :, 0:n, :],
                                     ACT.Copy).then_inc(p.sums_copied, 1)

            root(n0, 0)
            for g in range(GROUPS):
                if g + 1 < GROUPS:
                    root(n0, g + 1)
                normalize(n0, g)
                if g >= 2:
                    copy_t0(g - 2)
            copy_table(src_t, 0)
            copy_t0(GROUPS - 2)
            act.wait_ge(tr_copied, H)
            for k in range(GOT):
                take_list(p0, k, k)
            copy_t0(GROUPS - 1)
            copy_table(ew_t, 1)
            copy_table(rel_t, 2)

            def place(q, part, comp, stage, scale):
                rows_ = slice(MUL * part, MUL * (part + 1))
                dst_ = lin2[rows_, q, 0:MUL] if comp is None else lin2[rows_, q, MUL + comp:FEAT:3]
                nc.scalar.activation(dst_, stage[rows_, :], ACT.Copy, scale=scale).then_inc(lin2_ready, 1)

            def place_lin2():
                act.wait_ge(const, 8)
                act.wait_ge(w_in, 16 * N_WEIGHTS)
                place(3, 0, None, lin2_a, LIN2_SCALE)
                for i in range(3):
                    place(3, 1 + i, i, lin2_a, LIN2_SCALE)
                    place(i, 0, i, lin2_b, LIN2_SCALE)
                    place(i, 1 + i, None, lin2_b, LIN2_SCALE * INV_SQRT3)

            def hidden(i, s, r):
                act.wait_ge(xT_done, chunks_done(i, r))
                nc.scalar.activation(xT[:, s, :], psum[0:TILES * 8, 0, s * 128:(s + 1) * 128],
                                     ACT.Copy).then_inc(xT_copied, 1)
                act.wait_ge(hid_done, chunks_done(i, r))
                nc.scalar.activation(hid[:, s, :, :], psum[:, 1, :].rearrange("p (v e) -> p v e", e=128),
                                     ACT.Silu, scale=FC1_SCALE).then_inc(silu_done, 1)

            def edge_pass0(r, first_round):
                if not first_round:
                    for k in range(GOT):
                        take_list(p0, k, k)
                hidden(0, 0, r)
                if first_round:
                    for g in range(GROUPS):
                        leading_part(n0, g)

                def step(i, s, m, k, q, first=False, pick=True, more=True):
                    hidden(i + 1, 1 - s, r)
                    if first and first_round:
                        place_lin2()
                    before = (k - 1) % GOT
                    if s == 0 and pick:
                        copy_pick(p0, 128, 0, PICK_AT, m, r)
                    if not first:
                        act.wait_ge(p0.agg_done, chunks_done(i - 1, r))
                        if s == 0 and pick:
                            nc.scalar.activation(got[:, k + 1, PICK_T, :], psum[:, AGG0, ROWS_AT:ROWS_AT + FEAT],
                                                 ACT.Copy).then_inc(p0.picked_in, 1)
                        copy_sums(p0, COEF, SUMS0, AGG0, i - 1, before, r)
                    if more:
                        act.wait_ge(p0.gathered[k], tiles_in0(k, q, r))
                        act.wait_ge(prod_done, chunks_done(i, r))
                        take_list(p0, i + GOT, k)

                def tail():
                    hidden(LAST, 0, r)
                    copy_sums(p0, COEF, SUMS0, AGG0, LAST - 2, 2, r)
                    copy_sums(p0, COEF, SUMS0, AGG0, LAST - 1, 3, r)
                    copy_sums(p0, COEF, SUMS0, AGG0, LAST, 0, r)

                step(0, 0, 0, 0, 0, True, False)
                step(1, 1, 0, 1, 0)
                step(2, 0, 1, 2, 0)
                step(3, 1, 1, 3, 0)
                with act.Fori(1, QUADS - UNPICKED) as q:
                    for k in range(GOT):
                        step(q * GOT + k, k % 2, q * 2 + k // 2, k, q)
                for q in range(QUADS - UNPICKED, QUADS - 1):
                    for k in range(GOT):
                        step(q * GOT + k, k % 2, q * 2 + k // 2, k, q, pick=False)
                q = QUADS - 1
                step(LAST - 4, 0, PAIRS - 2, 0, q, pick=False)
                step(LAST - 3, 1, PAIRS - 2, 1, q, more=False)
                step(LAST - 2, 0, PAIRS - 1, 2, q, pick=False, more=False)
                tail()

            act.wait_ge(tables, 1)
            edge_pass0(0, True)
            many = act.value_load(general[0:1, 0:1], min_val=0, max_val=1)
            with act.If(many > 0):
                with act.Fori(1, WINDOWS) as r:
                    act.wait_ge(tables, r + 1)
                    edge_pass0(r, False)

            root(n1, 0)
            for g in range(GROUPS):
                if g + 1 < GROUPS:
                    root(n1, g + 1)
                normalize(n1, g)
            for g in range(GROUPS):
                leading_part(n1, g)

            def select(i, s):
                nc.scalar.activation(sel_c[:, s, :], ident_bf[0:CHUNKS, bass.ds(i, 1)].to_broadcast([CHUNKS, 32]),
                                     ACT.Copy).then_inc(sel_ready, 1)

            def copy_turned(m, r):
                act.wait_ge(turned, picks(p1, m, r))
                nc.scalar.activation(picked[:, :, :], psum[:, PICK_BANK, 256:512].rearrange("p (s f) -> p s f", s=2),
                                     ACT.Copy).then_inc(p1.picked_in, 1)

            def edge_pass1(r):
                for k in range(GOT):
                    take_list(p1, k, k)
                for k in range(GOT - 1):
                    select(k, k)
                copy_pick(p1, 256, PICK_BANK, 0, 0, r)

                def step(i, s, k, q, more=True, sel=True):
                    if sel:
                        act.wait_ge(typ_done, chunks_done(i, r))
                        select(i + 3, (k + 3) % GOT)
                    if more:
                        act.wait_ge(p1.gathered[k], tiles_in(k, q, r))
                        act.wait_ge(p1.agg_done, chunks_done(i, r))
                        take_list(p1, i + GOT, k)
                    copy_sums(p1, BASES, BASES, 4 + s, i, s, r)

                with act.Fori(0, QUADS - 1) as q:
                    for k in (0, 2):
                        m = q * 2 + k // 2
                        copy_turned(m, r)
                        step(q * GOT + k, 0, k, q)
                        copy_pick(p1, 256, PICK_BANK, 0, m + 1, r)
                        step(q * GOT + k + 1, 1, k + 1, q)
                q = QUADS - 1
                copy_turned(PAIRS - 2, r)
                step(LAST - 4, 0, 0, q)
                copy_pick(p1, 256, PICK_BANK, 0, PAIRS - 1, r)
                step(LAST - 3, 1, 1, q, more=False)
                copy_turned(PAIRS - 1, r)
                step(LAST - 2, 0, 2, q, more=False, sel=False)
                step(LAST - 1, 1, 3, q, more=False, sel=False)
                copy_sums(p1, BASES, BASES, 4, LAST, 0, r)

            edge_pass1(0)
            many = act.value_load(general[0:1, 0:1], min_val=0, max_val=1)
            with act.If(many > 0):
                with act.Fori(1, WINDOWS) as r:
                    act.wait_ge(tables1, r)
                    edge_pass1(r)

            act.wait_ge(sums_ready, 2)
            for g in range(GROUPS):
                for a, n in IN_BANKS:
                    cols = slice((g * GB + a) * NB, (g * GB + a + n) * NB)
                    nc.scalar.activation(acc_y[:, cols], acc[1][:, cols], ACT.Relu,
                                         bias=bias_c[:, :]).then_inc(y_relu, 1)

        @block.vector
        def _(dve):
            def statistics(n, g):
                if g:
                    dve.wait_ge(n.aggr, g * GB)
                for j in range(GB):
                    nc.vector.bn_stats(stats[:, j, :], xs[:, g * GB + j, :]).then_inc(n.stat, 1)
                for j in range(GB):
                    dve.wait_ge(n.stat, g * GB + j + 1)
                    nc.vector.bn_aggr(mv[:, g * GB + j, :], stats[:, j, :]).then_inc(n.aggr, 1)
                bl = slice(g * GB, (g + 1) * GB)
                dve.wait_ge(n.aggr, (g + 1) * GB)
                nc.vector.tensor_scalar_add(var_eps[:, bl], mv[:, bl, 1], EPS).then_inc(n.var, 1)

            def factors(n, g):
                bl = slice(g * GB, (g + 1) * GB)
                dve.wait_ge(n.root, g + 1)
                nc.vector.reciprocal(rstd[:, bl], std[:, bl]).then_inc(n.inv, 1)
                dve.wait_ge(n.inv, g + 1)
                nc.vector.scalar_tensor_tensor(out=nmr[:, bl], in0=mv[:, bl, 0], scalar=-1.0, in1=rstd[:, bl],
                                               op0=ALU.mult, op1=ALU.mult).then_inc(n.nmr, 1)

            def copy_hT(g):
                dve.wait_ge(tp_done, (g + 1) * GB)
                if g >= 2:
                    dve.wait_ge(t0_mm, (g - 1) * GB)
                for a, n in IN_BANKS:
                    nc.vector.tensor_copy(hT[:, g % 2, a:a + n, :],
                                          in_bank(a // 3, n)[:, :, 0:NB]).then_inc(hT_copied, 1)

            for g in range(GROUPS):
                dve.wait_ge(x_in[g], MOVED)
                statistics(n0, g)
                if g:
                    factors(n0, g - 1)
                if g >= 2:
                    copy_hT(g - 2)
            factors(n0, GROUPS - 1)
            copy_hT(GROUPS - 2)

            dve.wait_ge(cast, 2)
            nc.vector.tensor_copy(node_id[:, :], node_i[:, :]).then_inc(consts_f, 1)
            dve.wait_ge(const, 8)
            nc.vector.tensor_copy(iota_w[:, :], iota_i[:, :]).then_inc(consts_f, 1)
            nc.vector.tensor_copy(rel_id[:, :], rel_i[:, :]).then_inc(consts_f, 1)
            nc.vector.tensor_copy(ident_bf[:, :], ident[:, :]).then_inc(consts_f, 1)

            dve.wait_ge(dst_in, 32)
            nc.vector.tensor_copy(dst_f, dst_i).then_inc(d_step, 1)
            copy_hT(GROUPS - 1)
            dve.wait_ge(d_step, 1)
            halves = dst_f.rearrange("c (h e) -> c h e", h=H)
            nc.vector.tensor_reduce(dmax[:, :], halves, AX.X, ALU.max).then_inc(d_step, 1)
            nc.vector.tensor_scalar(dst_hi, dst_f, 0.0, PAD_HIGH, ALU.is_lt, ALU.mult).then_inc(d_step, 1)
            dve.wait_ge(d_step, 3)
            nc.vector.tensor_tensor(dst_hi, dst_hi, dst_f, ALU.add).then_inc(d_step, 1)
            dve.wait_ge(d_step, 4)
            nc.vector.tensor_reduce(dmin[:, :], dst_hi.rearrange("c (h e) -> c h e", h=H), AX.X,
                                    ALU.min).then_inc(d_step, 1)
            dve.wait_ge(d_step, 5)
            nc.vector.tensor_tensor(span[:, :], dmax[:, :], dmin[:, :], ALU.subtract).then_inc(d_step, 1)
            dve.wait_ge(d_step, 6)
            nc.vector.tensor_scalar(wide[:, :], span[:, :], float(WIN), None, ALU.is_ge).then_inc(d_step, 1)
            dve.wait_ge(d_step, 7)
            nc.vector.tensor_reduce(nwide[:, :], wide[:, :], AX.X, ALU.add).then_inc(d_step, 1)
            dve.wait_ge(cnt_done, 1)
            nc.vector.tensor_scalar(narrow[:, :], psum[:, 7, 0:1], 0.5, None, ALU.is_lt).then_inc(d_step, 1)
            nc.vector.tensor_scalar(general[:, :], psum[0:1, 7, 0:1], 0.5, None, ALU.is_gt).then_inc(d_step, 1)
            dve.wait_ge(d_step, 10)
            nc.vector.tensor_scalar(dmin[:, :], dmin[:, :], narrow[0:CHUNKS, :], None, ALU.mult).then_inc(d_step, 1)
            dve.wait_ge(d_step, 11)
            for h in range(H):
                nc.vector.tensor_scalar(dst_hi[:, h * HALF:(h + 1) * HALF], dst_f[:, h * HALF:(h + 1) * HALF],
                                        dmin[:, h:h + 1], None, ALU.subtract).then_inc(d_rows, 1)

            dve.wait_ge(min_done, 2)
            for h in range(H):
                nc.vector.tensor_copy(wmin_f[:, :, h], psum[0:1, 7, 128 * (h + 1):128 * (h + 1) + CHUNKS])\
                    .then_inc(d_step, 1)
            dve.wait_ge(d_step, 13)
            nc.vector.tensor_copy(wmin[:, :, :], wmin_f[:, :, :]).then_inc(d_step, 1)
            dve.wait_ge(d_step, 14)
            dve.wait_ge(tr_copied, 6)
            dve.wait_ge(acc_zero, 2)
            nc.vector.tensor_scalar_add(narrow[0:1, :], narrow[0:1, :], 0.0).then_inc(tables, 1)

            def one_hot(p, i, s, r, free):
                if free:
                    dve.wait_ge(p.agg_done, chunks_done(i - 2, r))
                rel = rel_t[:, bass.ds(i, 1), :].rearrange("p a t -> p (a t)").unsqueeze(2)
                nc.vector.tensor_tensor(onehot[:, s, :, :], rel.broadcast_to([128, TILES, WIN]),
                                        iota_w[:, :].unsqueeze(1).broadcast_to([128, TILES, WIN]),
                                        ALU.is_equal).then_inc(p.onehot, 1)

            def spread(p, coefs, n, s, i, r):
                dve.wait_ge(p.onehot, chunks_done(i, r))
                o = oc[:, s, 0:TILES * n * WIN].rearrange("p (t n w) -> p t n w", t=TILES, n=n)
                nc.vector.tensor_tensor(o, coefs.unsqueeze(3).broadcast_to([128, TILES, n, WIN]),
                                        onehot[:, s, :, :].unsqueeze(2).broadcast_to([128, TILES, n, WIN]),
                                        ALU.mult).then_inc(p.oc_done, 1)

            def accumulate(p, a, m, r, slots=None):
                slots = slots or p.per
                firsts = [dve.value_load(wmin[0:1, bass.ds(m * p.per + s, 1), h:h + 1].rearrange("p a b -> p (a b)"),
                                         min_val=0, max_val=NODES - 1) for s in range(slots) for h in range(H)]
                dve.wait_ge(p.out_done, outs_done(p, m, r))
                for n, first in enumerate(firsts):
                    if not (isinstance(m, int) and m == 0 and n == 0 and isinstance(r, int) and r == 0):
                        dve.wait_ge(p.acc_done, (r * CHUNKS + m * p.per) * H + n)
                    window = a[:, bass.ds(first, WIN)]
                    nc.vector.tensor_tensor(window, window, psum[:, OUT_BANK, n * WIN:(n + 1) * WIN],
                                            ALU.add).then_inc(p.acc_done, 1)

            def source_columns(p, u, n, r):
                if p is p1:
                    before = picks_before(p, u, r)
                elif isinstance(u, int) and u == 0:
                    before = picks_before(p, 1, r)
                else:
                    before = picks_before(p, u * 2, r)
                if not (isinstance(before, int) and before == 0):
                    dve.wait_ge(p.pick_done, before * 2 + n - 1)
                if p is p1:
                    sources = src_b[0:NB, bass.ds(u * 256, 256)].rearrange("p (s e) -> p s e", s=2)
                else:
                    sources = src_b[0:NB, bass.ds(u * 512, 512)].rearrange("p (s a e) -> p s a e", s=2, a=2)[:, :, 1, :]
                first, end = PICK_HALVES[n]
                for b in range(first, end):
                    last = nc.vector.tensor_scalar(is_src[:, b, :].rearrange("p (s e) -> p s e", s=2), sources,
                                                   node_id[:, b:b + 1], None, ALU.is_equal)
                last.then_inc(p.is_src_done, 1)

            def split(n, g):
                dve.wait_ge(n.hi_done, g + 1)
                bl = slice(g * GB, (g + 1) * GB)
                nc.vector.scalar_tensor_tensor(out=table_16[:, bl, 1, :], in0=hn[:, g, :, :], scalar=PICK_SCALE,
                                               in1=table_16[:, bl, 0, :], op0=ALU.mult,
                                               op1=ALU.subtract).then_inc(n.lo_done, 1)

            def edges0(i, s, m, k, q, r, loads=1, free=True, pick=False):
                one_hot(p0, i, s, r, free)
                dve.wait_ge(ea4_in[s], ea_loads(s, m, r, loads))
                spread(p0, ea4_c[:, s, :, :].rearrange("p h (k c) -> p (h k) c", c=COEF), COEF, s, i, r)
                dve.wait_ge(w_done, chunks_done(i, r))
                dve.wait_ge(p0.gathered[k], tiles_in0(k, q, r))
                w = psum[:, 2 + 2 * s:4 + 2 * s, :].rearrange("p b (t f) -> p (b t) f", f=128)
                w = w.rearrange("p t (j u) -> p t j u", u=MUL)
                if pick:
                    dve.wait_ge(p0.picked_in, picks(p0, m, r))
                products = prod[:, s, :, :].rearrange("p t (j n u) -> p t j n u", j=2, u=MUL)
                for part, j in enumerate((0, 2, 2, 2)):
                    o = products[:, :, :, part, :]
                    v = got[:, k, :, MUL * part:MUL * (part + 1)].unsqueeze(2).broadcast_to([128, TILES, 2, MUL])
                    last = nc.vector.tensor_tensor(o, w[:, :, j:j + 2, :], v, ALU.mult)
                last.then_inc(prod_done, 1)

            def edge_pass0(r):
                if isinstance(r, int):
                    for g in range(GROUPS):
                        split(n0, g)
                edges0(0, 0, 0, 0, 0, r, free=False)
                if isinstance(r, int):
                    for g in range(GROUPS):
                        split(n0, g)
                edges0(1, 1, 0, 1, 0, r, free=False)
                dve.wait_ge(src_b_in, 16)
                source_columns(p0, 0, 0, r)
                source_columns(p0, 0, 1, r)
                edges0(2, 0, 1, 2, 0, r)
                source_columns(p0, 1, 0, r)
                edges0(3, 1, 1, 3, 0, r, pick=True)
                source_columns(p0, 1, 1, r)

                def pair(m, k, q, columns, pick=True):
                    edges0(m * 2, 0, m, k, q, r)
                    if columns:
                        source_columns(p0, q + 1, 0, r)
                    edges0(m * 2 + 1, 1, m, k + 1, q, r, pick=pick)
                    if columns:
                        source_columns(p0, q + 1, 1, r)

                def quad(q, columns, pick=True):
                    pair(q * 2, 0, q, False, pick)
                    accumulate(p0, acc[0], q - 1, r)
                    pair(q * 2 + 1, 2, q, columns, pick)

                last_picked = QUADS - UNPICKED - 1
                quad(1, True)
                with dve.Fori(2, last_picked) as q:
                    quad(q, True)
                quad(last_picked, False)
                for q in range(last_picked + 1, QUADS):
                    quad(q, False, False)
                edges0(LAST, 0, PAIRS, 0, QUADS, r, 3)
                accumulate(p0, acc[0], QUADS - 1, r)
                accumulate(p0, acc[0], QUADS, r, 1)
                dve.wait_ge(p0.acc_done, H * chunks_done(LAST, r))

            def shift_windows(by):
                nc.vector.tensor_scalar_add(rel_t[:, :, :], rel_t[:, :, :], float(-by)).then_inc(shifted, 1)
                nc.vector.tensor_scalar_add(wmin_f[:, :, :], wmin_f[:, :, :], float(by)).then_inc(shifted, 1)

            many = dve.value_load(general[0:1, 0:1], min_val=0, max_val=1)
            edge_pass0(0)
            with dve.If(many > 0):
                with dve.Fori(1, WINDOWS) as r:
                    shift_windows(WIN)
                    dve.wait_ge(shifted, r * 3 - 1)
                    nc.vector.tensor_copy(wmin[:, :, :], wmin_f[:, :, :]).then_inc(shifted, 1)
                    dve.wait_ge(shifted, r * 3)
                    nc.vector.tensor_scalar_add(narrow[0:1, :], narrow[0:1, :], 0.0).then_inc(tables, 1)
                    edge_pass0(r)

            dve.sem_inc(sums_ready, 1)

            def add_transposed(g, transposed, to, other, added):
                for a, n in IN_BANKS:
                    dve.wait_ge(transposed, g * GB + a + n)
                    bl = slice(g * GB + a, g * GB + a + n)
                    nc.vector.tensor_tensor(to(g, a, n), in_bank(2 * (g % 4) + a // 3, n)[0:NB, :, :], other[:, bl, :],
                                            ALU.add).then_inc(added, 1)

            for g in range(GROUPS):
                add_transposed(g, l0_tp, lambda g, a, n: xs[:, g * GB + a:g * GB + a + n, :], xs, l0_add)
                dve.wait_ge(l0_add, 2 * (g + 1))
                statistics(n1, g)
                if g:
                    factors(n1, g - 1)
            factors(n1, GROUPS - 1)
            for g in range(GROUPS):
                split(n1, g)

            def type_rows(i, s, r):
                dve.wait_ge(typ_done, chunks_done(i, r))
                nc.vector.tensor_scalar(typ1[:, s, :], psum[:, 2 * s, 0:H * 128], rel_id[:, :], None,
                                        ALU.is_equal).then_inc(typ1_done, 1)

            def edges1(i, s, m, r, free=True):
                one_hot(p1, i, s, r, free)
                dve.wait_ge(cf_done, chunks_done(i, r))
                cf = psum[:, 1 + 2 * s, 0:TILES * BASES].rearrange("p (t b) -> p t b", b=BASES)
                ew = ew_t[:, bass.ds(i, 1), :].rearrange("p a t -> p (a t)").unsqueeze(2)
                nc.vector.tensor_tensor(coef[:, s, :, :], cf, ew.broadcast_to([128, TILES, BASES]),
                                        ALU.mult).then_inc(coef_done, 1)
                dve.wait_ge(coef_done, chunks_done(i, r))
                spread(p1, coef[:, s, :, :], BASES, s, i, r)

            def edge_pass1(r):
                def pair(m, pick=True):
                    edges1(m * 2, 0, m, r)
                    type_rows(m * 2 + 1, 1, r)
                    if pick:
                        source_columns(p1, m + 1, 0, r)
                    edges1(m * 2 + 1, 1, m, r)
                    type_rows(m * 2 + 2, 0, r)
                    if pick:
                        source_columns(p1, m + 1, 1, r)
                    accumulate(p1, acc[1], m - 1, r)

                type_rows(0, 0, r)
                type_rows(1, 1, r)
                source_columns(p1, 0, 0, r)
                source_columns(p1, 0, 1, r)
                edges1(0, 0, 0, r, False)
                edges1(1, 1, 0, r, False)
                source_columns(p1, 1, 0, r)
                source_columns(p1, 1, 1, r)
                type_rows(2, 0, r)
                pair(1)
                with dve.Fori(2, PAIRS - 1) as m:
                    pair(m)
                pair(PAIRS - 1, False)
                edges1(LAST, 0, PAIRS, r)
                accumulate(p1, acc[1], PAIRS - 1, r)
                accumulate(p1, acc[1], PAIRS, r, 1)
                dve.wait_ge(p1.acc_done, H * chunks_done(LAST, r))

            many = dve.value_load(general[0:1, 0:1], min_val=0, max_val=1)
            edge_pass1(0)
            with dve.If(many > 0):
                with dve.Fori(1, WINDOWS) as r:
                    shift_windows(-WIN)
                    dve.wait_ge(shifted, 3 * (WINDOWS - 1) + r * 3 - 1)
                    nc.vector.tensor_copy(wmin[:, :, :], wmin_f[:, :, :]).then_inc(shifted, 1)
                    dve.wait_ge(shifted, 3 * (WINDOWS - 1) + r * 3)
                    nc.vector.tensor_scalar_add(narrow[0:1, :], narrow[0:1, :], 0.0).then_inc(tables1, 1)
                    edge_pass1(r)

            dve.sem_inc(sums_ready, 1)

            for g in range(GROUPS):
                add_transposed(g, y_tp, lambda g, a, n: hn[:, g, a:a + n, :], xs, y_add)

        @block.tensor
        def _(pe):
            pe.wait_ge(const, 1)

            def transpose_group(g):
                pe.wait_ge(n0.normed, (g + 1) * GB)
                if g:
                    pe.wait_ge(hT_copied, 2 * g)
                for j in range(GB):
                    nc.tensor.transpose(in_bank(j // 3, 3)[:, j % 3, 0:NB], hn[:, g, j, :],
                                        ident[0:NB, 0:NB]).then_inc(tp_done, 1)

            def lin1_group(g):
                pe.wait_ge(hT_copied, 2 * (g + 1))
                if g:
                    pe.wait_ge(t0_rows, 2 * g)
                for j in range(GB):
                    nc.tensor.matmul(in_bank(2 + j // 3, 3)[0:NB, j % 3, :], hT[:, g % 2, j, :], lin1[:, :],
                                     start=True, stop=True).then_inc(t0_mm, 1)

            def count_wide():
                pe.wait_ge(d_step, 8)
                nc.tensor.matmul(psum[:, 7, 0:1], ones[0:CHUNKS, :], nwide[:, :], start=True, stop=True)\
                    .then_inc(cnt_done, 1)

            def turn_rows(row, n):
                for h in range(H):
                    if n:
                        pe.wait_ge(tr_copied, H * (n - 1) + h + 1)
                    for k in range(K):
                        nc.tensor.transpose(psum[:, 5 + h, k * CHUNKS:(k + 1) * CHUNKS],
                                            row[:, h * HALF + k:(h + 1) * HALF:K],
                                            ident[0:CHUNKS, 0:CHUNKS]).then_inc(tr_done, 1)

            transpose_group(0)
            pe.wait_ge(cast, 1)
            turn_rows(src_f, 0)
            pe.wait_ge(lin1_in, 16 * 4)
            for g in range(1, GROUPS):
                transpose_group(g)
                lin1_group(g - 1)
            lin1_group(GROUPS - 1)
            pe.wait_ge(ew_in, 32)
            turn_rows(ew_f, 1)
            count_wide()
            pe.wait_ge(d_rows, 2)
            turn_rows(dst_hi, 2)
            for h in range(H):
                nc.tensor.transpose(psum[0:1, 7, 128 * (h + 1):128 * (h + 1) + CHUNKS], dmin[:, h:h + 1],
                                    ident[0:CHUNKS, 0:CHUNKS]).then_inc(min_done, 1)

            def turn_attributes(i, s, m, r, loads=1):
                pe.wait_ge(ea8_in[s], ea_loads(s, m, r, loads))
                pe.sem_inc(turn_turn, 1)
                nc.tensor.transpose(psum[0:TILES * 8, 0, s * 128:(s + 1) * 128],
                                    ea8_c[:, s, :, :].rearrange("p h c -> p (h c)"), ident[:, :]).then_inc(xT_done, 1)

            def hidden(i, s, r):
                pe.wait_ge(xT_copied, chunks_done(i, r))
                for v in range(TILES // 2):
                    last = nc.tensor.matmul(psum[:, 1, v * 128:(v + 1) * 128], fc1_bd[:, v, :], xT[:, s, :],
                                            start=True, stop=True)
                last.then_inc(hid_done, 1)

            def edge_weights(i, s, r, free):
                pe.wait_ge(silu_done, chunks_done(i, r))
                if free:
                    pe.wait_ge(prod_done, chunks_done(i - 2, r))
                for v in range(TILES // 2):
                    last = nc.tensor.matmul(psum[:, 2 + 2 * s + v // 2, (v % 2) * 256:(v % 2 + 1) * 256],
                                            hid[:, s, v, :], fc2_bd[:, :], start=True, stop=True)
                last.then_inc(w_done, 1)

            def pick(p, m, n, bank, at, r, columns):
                c, cols, written = columns
                before = picks_before(p, m, r)
                if n == 0 and not (isinstance(before, int) and before == 0):
                    pe.wait_ge(p.picked_in, before)
                if n == 0 and isinstance(before, int) and before == 0:
                    pe.wait_ge((n1 if p is p1 else n0).lo_done, GROUPS)
                pe.wait_ge(p.is_src_done, written * 2 + n + 1)
                first, end = PICK_HALVES[n]
                for b in range(first, end):
                    for part in range(2):
                        last = nc.tensor.matmul(psum[:, bank, at:at + cols], table_16[:, b, part, :],
                                                is_src[:, b, c:c + cols], start=(b == 0 and part == 0),
                                                stop=(b == BLOCKS - 1 and part == 1))
                last.then_inc(p.pick_done, 1)

            def sums0(i, s, r, free, picked_pair=None):
                pe.wait_ge(prod_done, chunks_done(i, r))
                pe.wait_ge(p0.oc_done, chunks_done(i, r))
                if free:
                    pe.wait_ge(p0.sums_copied, chunks_done(i - 1, r))
                for h in range(H):
                    for a, q0, qn, to in ((128, 1, 3, 0), (0, 0, COEF, 3)):
                        o = (h * SUMS0 + to) * WIN
                        for k in range(K):
                            t = h * K + k
                            c = (t * COEF + q0) * WIN
                            last = nc.tensor.matmul(psum[:, AGG0, o:o + qn * WIN], prod[:, s, t, a:a + 128],
                                                    oc[:, s, c:c + qn * WIN], start=(k == 0), stop=(k == K - 1))
                if picked_pair is not None:
                    pe.wait_ge(p0.pickT_copied, picks(p0, picked_pair, r))
                    last = nc.tensor.matmul(psum[:, AGG0, ROWS_AT:ROWS_AT + FEAT], pickT[:, 0:128], lin1[:, :],
                                            start=True, stop=True)
                last.then_inc(p0.agg_done, 1)

            def outputs(p, n, w, m, r, slots=None):
                slots = slots or p.per
                pe.wait_ge(p.sums_copied, r * CHUNKS + m * p.per + slots)
                if not (isinstance(m, int) and m == 0):
                    pe.wait_ge(p.acc_done, (r * CHUNKS + m * p.per) * H)
                for q in range(n):
                    last = nc.tensor.matmul(psum[:, OUT_BANK, 0:slots * H * WIN], w[:, q, :],
                                            p.sums[:, q, 0:slots, :, :].rearrange("p s h w -> p (s h w)"),
                                            start=(q == 0), stop=(q == n - 1))
                last.then_inc(p.out_done, 1)

            def edge_pass0(r):
                turn_attributes(0, 0, 0, r)
                hidden(0, 0, r)
                turn_attributes(1, 1, 0, r)
                edge_weights(0, 0, r, False)
                hidden(1, 1, r)
                turn_attributes(2, 0, 1, r)
                edge_weights(1, 1, r, False)
                hidden(2, 0, r)
                sums0(0, 0, r, False)

                def even(m, odd_pair, q, picks=True):
                    turn_attributes(m * 2 + 1, 1, m, r)
                    edge_weights(m * 2, 0, r, True)
                    hidden(m * 2 + 1, 1, r)
                    if picks:
                        for n in range(2):
                            pick(p0, m, n, 0, PICK_AT, r, (128 * odd_pair, 128, r * (QUADS - UNPICKED) + q))
                    sums0(m * 2 - 1, 1, r, True, m if picks else None)

                def odd(m, q=None, loads=1):
                    turn_attributes(m * 2 + 2, 0, m + 1, r, loads)
                    edge_weights(m * 2 + 1, 1, r, True)
                    if q is not None:
                        outputs(p0, COEF, lin2, q, r)
                    hidden(m * 2 + 2, 0, r)
                    sums0(m * 2, 0, r, True)

                even(1, 1, 0)
                odd(1)
                if isinstance(r, int):
                    pe.wait_ge(lin2_ready, 10)

                def quad(q, picks=True):
                    even(q * 2, 0, q, picks)
                    odd(q * 2, q - 1)
                    even(q * 2 + 1, 1, q, picks)
                    odd(q * 2 + 1)

                quad(1)
                with pe.Fori(2, QUADS - UNPICKED) as q:
                    quad(q)
                for q in range(QUADS - UNPICKED, QUADS - 1):
                    quad(q, False)
                even(PAIRS - 2, 0, QUADS - 1, False)
                odd(PAIRS - 2, QUADS - 2)
                even(PAIRS - 1, 1, QUADS - 1, False)
                odd(PAIRS - 1, None, 3)
                edge_weights(LAST, 0, r, True)
                sums0(LAST - 1, 1, r, True)
                outputs(p0, COEF, lin2, QUADS - 1, r)
                sums0(LAST, 0, r, True)
                outputs(p0, COEF, lin2, QUADS, r, 1)

            pe.wait_ge(w_in, 16 * N_WEIGHTS)
            pe.wait_ge(tables, 1)
            edge_pass0(0)
            many = pe.value_load(general[0:1, 0:1], min_val=0, max_val=1)
            with pe.If(many > 0):
                with pe.Fori(1, WINDOWS) as r:
                    pe.wait_ge(tables, r + 1)
                    edge_pass0(r)

            def turn_blocks(t, g, done, added, ready=None):
                if g >= 4:
                    pe.wait_ge(added, 2 * (g - 3))
                for j in range(GB):
                    if ready is not None and j in (0, 3):
                        pe.wait_ge(ready, 2 * g + (1 if j == 0 else 2))
                    b = g * GB + j
                    nc.tensor.transpose(in_bank(2 * (g % 4) + j // 3, 3)[0:NB, j % 3, :], t[:, b * NB:(b + 1) * NB],
                                        ident[:, :]).then_inc(done, 1)

            pe.wait_ge(sums_ready, 1)
            for g in range(GROUPS):
                turn_blocks(acc[0], g, l0_tp, l0_add)

            def spread_types(i, s, k4, r):
                pe.wait_ge(sel_ready, chunks_done(i, r))
                for k in range(K):
                    last = nc.tensor.matmul(psum[32 * k:32 * k + 32, 2 * s, 0:H * 128], sel_c[:, k4, :],
                                            et_rows[:, k:CHUNK:K], start=True, stop=True)
                last.then_inc(typ_done, 1)

            def coefficients(i, s, r):
                pe.wait_ge(typ1_done, chunks_done(i, r))
                for h in range(H):
                    last = nc.tensor.matmul(psum[:, 1 + 2 * s, 32 * h:32 * (h + 1)],
                                            typ1[:, s, 128 * h:128 * (h + 1)], wc_bd[:, :], start=True, stop=True)
                last.then_inc(cf_done, 1)

            def sums1(i, s, m, k4, q, r, free, last_chunk=False):
                if last_chunk:
                    pe.wait_ge(p1.gathered[0], tiles_in(0, QUADS, r) + 16)
                else:
                    pe.wait_ge(p1.gathered[k4], tiles_in(k4, q, r))
                    pe.wait_ge(p1.picked_in, picks(p1, m, r))
                pe.wait_ge(p1.oc_done, chunks_done(i, r))
                if free:
                    pe.wait_ge(p1.sums_copied, chunks_done(i - 2, r))
                n = BASES * WIN
                for h in range(H):
                    for k in range(K):
                        t = h * K + k
                        rows_ = got[:, k4, t, :] if t != PICK_T or last_chunk else picked[:, s, :]
                        last = nc.tensor.matmul(psum[:, 4 + s, h * n:(h + 1) * n], rows_,
                                                oc[:, s, t * n:(t + 1) * n], start=(k == 0), stop=(k == K - 1))
                last.then_inc(p1.agg_done, 1)

            def turn_picked(m, r):
                pe.wait_ge(p1.pickT_copied, picks(p1, m, r))
                for s in range(2):
                    last = nc.tensor.transpose(psum[:, PICK_BANK, 256 + 128 * s:256 + 128 * (s + 1)],
                                               pickT[:, 128 * s:128 * (s + 1)], ident[:, :])
                last.then_inc(turned, 1)

            def edge_pass1(r):
                def pick1(m, n):
                    pick(p1, m, n, PICK_BANK, 0, r, (0, 256, r * PAIRS + m))

                spread_types(0, 0, 0, r)
                spread_types(1, 1, 1, r)
                coefficients(0, 0, r)
                pick1(0, 0)
                pick1(0, 1)
                turn_picked(0, r)
                spread_types(2, 0, 2, r)
                coefficients(1, 1, r)
                pick1(1, 0)
                sums1(0, 0, 0, 0, 0, r, False)
                pick1(1, 1)

                def even(m, k, q, free=True):
                    spread_types(m * 2 + 1, 1, k + 1, r)
                    coefficients(m * 2, 0, r)
                    sums1(m * 2 - 1, 1, m - 1, (k - 1) % GOT, q - (k == 0), r, free)
                    turn_picked(m, r)

                def odd(m, k, q, more=True):
                    spread_types(m * 2 + 2, 0, (k + 2) % GOT, r)
                    coefficients(m * 2 + 1, 1, r)
                    outputs(p1, BASES, w_base, m - 1, r)
                    if more:
                        pick1(m + 1, 0)
                    sums1(m * 2, 0, m, k, q, r, True)
                    if more:
                        pick1(m + 1, 1)

                even(1, 2, 0, False)
                odd(1, 2, 0)
                with pe.Fori(1, QUADS - 1) as q:
                    for k in (0, 2):
                        even(q * 2 + k // 2, k, q)
                        odd(q * 2 + k // 2, k, q)
                q = QUADS - 1
                even(PAIRS - 2, 0, q)
                odd(PAIRS - 2, 0, q)
                even(PAIRS - 1, 2, q)
                odd(PAIRS - 1, 2, q, False)
                coefficients(LAST, 0, r)
                sums1(LAST - 1, 1, PAIRS - 1, 3, q, r, True)
                outputs(p1, BASES, w_base, PAIRS - 1, r)
                sums1(LAST, 0, PAIRS, 0, QUADS, r, True, True)
                outputs(p1, BASES, w_base, PAIRS, r, 1)

            pe.wait_ge(w1_in, 16 * (K + 3))
            edge_pass1(0)
            many = pe.value_load(general[0:1, 0:1], min_val=0, max_val=1)
            with pe.If(many > 0):
                with pe.Fori(1, WINDOWS) as r:
                    pe.wait_ge(tables1, r)
                    edge_pass1(r)

            for g in range(GROUPS):
                turn_blocks(acc_y, g, y_tp, y_add, y_relu)


_INS = ["x", "src", "dst", "edge_attr_4", "edge_attr_8", "edge_type_32", "edge_weight1", "L0_gnn_w_lin1_s",
        "L0_gnn_w_lin1_v", "L0_gnn_fc_w1", "L0_gnn_fc_w2", "L0_gnn_w_lin2_s", "L0_gnn_w_lin2_v",
        "L1_gnn_weight", "L1_gnn_w_comp", "L1_gnn_bias_param"]


def kernel(**inputs):
    import numpy as _np
    import concourse.bacc as _bacc
    from concourse.bass_utils import run_bass_kernel_spmd as _run

    nc = _bacc.Bacc("TRN2", target_bir_lowering=False, num_devices=1)
    arrays, args = {}, []
    for name in _INS:
        a = _np.ascontiguousarray(inputs[name])
        if name == "edge_weight1":
            a = a.reshape(-1)
        arrays[f"in_{name}"] = a
        args.append(nc.dram_tensor(f"in_{name}", a.shape, mybir.dt.from_np(a.dtype), kind="ExternalInput").ap())
    for name in ("table0", "table1"):
        args.append(nc.dram_tensor(name, [NODES, FEAT], FP32, kind="Internal").ap())
    args.append(nc.dram_tensor("src_row", [CHUNKS * 128], FP16, kind="Internal").ap())
    args.append(nc.dram_tensor("out_0", [NODES, FEAT], FP32, kind="ExternalOutput").ap())
    gnn_two_layers(nc, *args)
    r = _run(nc, [arrays], core_ids=[0])
    return r.results[0]["out_0"]
```
